# Optimizing a Trainium2 kernel written in Bass

```python
import numpy as np
import jax
import jax.numpy as jnp

def _softmax(x, axis=-1):
    return jax.nn.softmax(x, axis=axis)

def _gelu(x):
    return jax.nn.gelu(x, approximate=True)

def _silu(x):
    return jax.nn.silu(x)

def _sigmoid(x):
    return jax.nn.sigmoid(x)

def _layernorm(x, axis=-1, eps=1e-05):
    m = jnp.mean(x, axis=axis, keepdims=True)
    v = jnp.var(x, axis=axis, keepdims=True)
    return (x - m) / jnp.sqrt(v + eps)

def _scatter_add(tgt, idx, src, axis=0):
    return tgt.at[idx].add(src)

def _segment_sum(src, seg, n):
    return jax.ops.segment_sum(src, seg, n)
kernel_name = 'mk_gnn_preln_d2_gnn_r64_529822'

def setup_inputs(seed: int=0):
    np.random.seed(seed)
    _w = jnp.asarray

    def _rec_inputs():
        import jax
        import jax.numpy as jnp
        _gk = jax.random.key(seed)
        x = -0.000202 + 1 * jax.random.normal(jax.random.fold_in(_gk, 1), (100000, 64), jnp.float32)
        src = jax.random.randint(jax.random.fold_in(_gk, 2), (25000,), 0, 100000, jnp.int32)
        dst = jnp.minimum((100000 * jax.random.uniform(jax.random.fold_in(_gk, 3), (25000,)) ** 2.0).astype(jnp.int32), 99999)
        _o = jnp.argsort(dst, stable=True)
        src = src[_o]
        dst = dst[_o]
        edge_attr_32 = 0.000196303 + 1.00016 * jax.random.normal(jax.random.fold_in(_gk, 11), (25000, 32), jnp.float32)
        return (x, src, dst, edge_attr_32)
    x, src, dst, edge_attr_32 = _rec_inputs()

    def _L0_gnn_setup():
        import jax, jax.numpy as jnp
        import numpy as np
        N_NODES = 100000
        D_IN = 64
        D_HID = 128
        key = jax.random.key(seed)
        k_x, k_e, k_w1, k_b1, k_w2, k_b2 = jax.random.split(key, 6)
        x = jax.random.normal(k_x, (N_NODES, D_IN), dtype=jnp.float32)
        edge_index = jax.random.randint(k_e, (2, 25000), 0, N_NODES, dtype=jnp.int64)
        s1 = 1.0 / np.sqrt(D_IN)
        s2 = 1.0 / np.sqrt(D_HID)
        W1 = jax.random.uniform(k_w1, (D_IN, D_HID), jnp.float32, -s1, s1)
        b1 = jax.random.uniform(k_b1, (D_HID,), jnp.float32, -s1, s1)
        W2 = jax.random.uniform(k_w2, (D_HID, D_IN), jnp.float32, -s2, s2)
        b2 = jax.random.uniform(k_b2, (D_IN,), jnp.float32, -s2, s2)
        return {'x': x, 'edge_index': edge_index, 'W1': W1, 'b1': b1, 'W2': W2, 'b2': b2}
    _L0_gnn_all = _L0_gnn_setup()
    _L0_gnn_in = {k: v for k, v in _L0_gnn_all.items() if k in ('W1', 'b1', 'W2', 'b2')}
    del _L0_gnn_all

    def _L1_gnn_setup():
        import jax, jax.numpy as jnp
        import numpy as np
        N, D, E, ED, L = (100000, 64, 12500, 32, 5)
        LN_EPS = 1e-05

        def _leaky(x):
            return jax.nn.leaky_relu(x, negative_slope=0.1)
        key = jax.random.key(seed)
        ks = jax.random.split(key, 16)
        s = 0.05
        return {'x': jax.random.normal(ks[0], (N, D), dtype=jnp.float32), 'edge_index': jax.random.randint(ks[1], (2, E), 0, N, dtype=jnp.int64), 'edge_attr': jax.random.normal(ks[2], (E, ED), dtype=jnp.float32), 'W1': jax.random.normal(ks[3], (L, D, 2 * D), dtype=jnp.float32) * s, 'b1': jnp.zeros((L, 2 * D), dtype=jnp.float32), 'W2': jax.random.normal(ks[4], (L, 2 * D, D), dtype=jnp.float32) * s, 'b2': jnp.zeros((L, D), dtype=jnp.float32), 'We1': jax.random.normal(ks[5], (L, ED, D), dtype=jnp.float32) * s, 'be1': jnp.zeros((L, D), dtype=jnp.float32), 'We2': jax.random.normal(ks[6], (L, D, D), dtype=jnp.float32) * s, 'be2': jnp.zeros((L, D), dtype=jnp.float32), 'res_w': jnp.ones((L,), dtype=jnp.float32), 'dot_scale': jnp.ones((L,), dtype=jnp.float32), 'ln_g': jnp.ones((L, D), dtype=jnp.float32), 'ln_b': jnp.zeros((L, D), dtype=jnp.float32)}
    _L1_gnn_all = _L1_gnn_setup()
    _L1_gnn_in = {k: v for k, v in _L1_gnn_all.items() if k in ('W1', 'b1', 'W2', 'b2', 'We1', 'be1', 'We2', 'be2', 'res_w', 'dot_scale', 'ln_g', 'ln_b')}
    del _L1_gnn_all
    return {'x': x, 'src': src, 'dst': dst, 'edge_attr_32': edge_attr_32, 'L0_gnn_W1': _L0_gnn_in['W1'], 'L0_gnn_b1': _L0_gnn_in['b1'], 'L0_gnn_W2': _L0_gnn_in['W2'], 'L0_gnn_b2': _L0_gnn_in['b2'], 'L1_gnn_W1': _L1_gnn_in['W1'], 'L1_gnn_b1': _L1_gnn_in['b1'], 'L1_gnn_W2': _L1_gnn_in['W2'], 'L1_gnn_b2': _L1_gnn_in['b2'], 'L1_gnn_We1': _L1_gnn_in['We1'], 'L1_gnn_be1': _L1_gnn_in['be1'], 'L1_gnn_We2': _L1_gnn_in['We2'], 'L1_gnn_be2': _L1_gnn_in['be2'], 'L1_gnn_res_w': _L1_gnn_in['res_w'], 'L1_gnn_dot_scale': _L1_gnn_in['dot_scale'], 'L1_gnn_ln_g': _L1_gnn_in['ln_g'], 'L1_gnn_ln_b': _L1_gnn_in['ln_b']}

def reference(x, src, dst, edge_attr_32, L0_gnn_W1, L0_gnn_b1, L0_gnn_W2, L0_gnn_b2, L1_gnn_W1, L1_gnn_b1, L1_gnn_W2, L1_gnn_b2, L1_gnn_We1, L1_gnn_be1, L1_gnn_We2, L1_gnn_be2, L1_gnn_res_w, L1_gnn_dot_scale, L1_gnn_ln_g, L1_gnn_ln_b):
    import jax
    import jax.numpy as jnp

    def _L0_gnn_ref(x, edge_index, W1, b1, W2, b2):
        import jax, jax.numpy as jnp
        import numpy as np
        N_NODES = 100000
        D_IN = 64
        D_HID = 128
        row, col = (edge_index[0], edge_index[1])
        agg = jax.ops.segment_sum(x[col], row, num_segments=x.shape[0])
        out = agg + x
        h = jax.nn.relu(out @ W1 + b1)
        return h @ W2 + b2

    def _L1_gnn_ref(x, edge_index, edge_attr, W1, b1, W2, b2, We1, be1, We2, be2, res_w, dot_scale, ln_g, ln_b):
        import jax, jax.numpy as jnp
        import numpy as np
        N, D, E, ED, L = (100000, 64, 12500, 32, 5)
        LN_EPS = 1e-05

        def _leaky(x):
            return jax.nn.leaky_relu(x, negative_slope=0.1)
        src, dst = (edge_index[0], edge_index[1])
        n = x.shape[0]
        for l in range(W1.shape[0]):
            h = _leaky(x @ W1[l] + b1[l]) @ W2[l] + b2[l]
            e = _leaky(edge_attr @ We1[l] + be1[l]) @ We2[l] + be2[l]
            msg = h[src] * e * dot_scale[l]
            agg = jax.ops.segment_sum(msg, dst, num_segments=n)
            out = x + agg * res_w[l]
            mu = jnp.mean(out, axis=-1, keepdims=True)
            var = jnp.mean(jnp.square(out - mu), axis=-1, keepdims=True)
            x = (out - mu) * jax.lax.rsqrt(var + LN_EPS) * ln_g[l] + ln_b[l]
        return x
    edge_index = jnp.stack([src, dst])
    h = jnp.maximum(_layernorm(x, axis=-1), 0.0)
    x = x + _L0_gnn_ref(h, edge_index, L0_gnn_W1, L0_gnn_b1, L0_gnn_W2, L0_gnn_b2)
    h = jnp.maximum(_layernorm(x, axis=-1), 0.0)
    x = x + _L1_gnn_ref(h, edge_index, edge_attr_32, L1_gnn_W1, L1_gnn_b1, L1_gnn_W2, L1_gnn_b2, L1_gnn_We1, L1_gnn_be1, L1_gnn_We2, L1_gnn_be2, L1_gnn_res_w, L1_gnn_dot_scale, L1_gnn_ln_g, L1_gnn_ln_b)
    return x

_drawn_inputs = setup_inputs


def setup_inputs(seed=0):
    import zlib

    import numpy as np

    out = dict(_drawn_inputs(seed))
    spreads = {'L1_gnn_b1': (0.0, 0.8),
     'L1_gnn_b2': (0.0, 0.621),
     'L1_gnn_be1': (0.0, 2.0),
     'L1_gnn_be2': (0.0, 2.0),
     'L1_gnn_res_w': (1.0, 0.6),
     'L1_gnn_dot_scale': (1.0, 0.6),
     'L1_gnn_ln_g': (1.0, 0.2),
     'L1_gnn_ln_b': (0.0, 0.1)}
    factors = {'edge_attr_32': 6.361,
     'L1_gnn_W1': 4.695,
     'L1_gnn_W2': 3.852,
     'L1_gnn_We1': 6.471,
     'L1_gnn_We2': 5.064}
    for name, (base, spread) in spreads.items():
        noise = np.random.default_rng([zlib.crc32(name.encode()), seed]).standard_normal(out[name].shape)
        drawn = base * np.exp(spread * noise) if base else spread * noise
        out[name] = jnp.asarray(drawn.astype(out[name].dtype))
    for name, factor in factors.items():
        out[name] = (out[name] * factor).astype(out[name].dtype)
    return out
```

```python
import concourse.bass as bass
from concourse import mybir
from contextlib import ExitStack, contextmanager

fp32 = mybir.dt.float32
i32 = mybir.dt.int32
ALU = mybir.AluOpType
ACT = mybir.ActivationFunctionType
AX = mybir.AxisListType

N = 100000
E = 25000
F = 64
HID = 128
EF = 32
L = 5
EPS = 1e-5
ACT_SET = "natural_log_exp_and_others"
SLOPE = 0.1

P = 128
ET = 8
BE = ET * P
BODIES = -(-E // BE)
EP = BODIES * BE
GRP = BE // 2
LIVE = -(-(E - (BODIES - 1) * BE) // P)
TILES = EP // P
HT = TILES // 2
PADV = 131071
FAR = 1 << 20
ROWS = BODIES * P * 2 * ET

NB = 8
FULL = N // (P * NB)
TAIL = (N - FULL * P * NB) // NB
CP = 125
CHAIN = CP * NB
CC = CHAIN // 2

W1_C, W2_C, E1_C, E2_C, G_C, B_C, BIAS_C = 0, 128, 192, 320, 448, 512, 576
WC = BIAS_C + 4


CREDIT = 4


class Body:

    def __init__(self, eng, c, j, count, layer):
        self.eng, self.i, self.u, self.w, self.known = eng, j * 4 + c, c % 2, c % 4, {}
        self.c, self.j, self.count, self.layer = c, j, count, layer

    def value(self, key, x):
        if key not in self.known:
            self.known[key] = x if isinstance(x, int) else self.eng.snap(x)
        return self.known[key]

    def at(self, back, skip=0):
        return self.value(("at", back, skip), (self.layer - skip) * self.count + self.i + 1 + CREDIT - back)

    now = property(lambda self: self.at(0))
    prev = property(lambda self: self.at(1))
    older = property(lambda self: self.at(2))
    oldest = property(lambda self: self.at(4))

    def part(self, q, m, back=0):
        return self.value(("part", q, m, back), (self.layer * self.count + self.i + CREDIT - back) * m + q + 1)

    def in2(self, m=1, more=0, skip=0):
        uses = (self.layer - skip) * ((self.count + 1 - self.u) // 2) + self.j * 2 + self.c // 2 + 1
        return self.value(("in2", m, more, skip), uses * (16 * m) + 16 * more)

    def in4(self, m=1, more=0, skip=0):
        uses = (self.layer - skip) * ((self.count + 3 - self.w) // 4) + self.j + self.c // 4 + 1
        return self.value(("in4", m, more, skip), uses * (16 * m) + 16 * more)


def staged(eng, count, *stages, layer=0):
    top = max(ahead for ahead, _ in stages)

    def beside(c, j, lo, hi):
        bodies = {}
        for ahead, step in stages:
            if lo <= c + ahead < hi:
                if ahead not in bodies:
                    bodies[ahead] = Body(eng, c + ahead, j, count, layer)
                step(bodies[ahead])

    turns = (count - top) // 4
    for c in range(-top, 0):
        beside(c, 0, 0, count)
    with eng.Fori(0, turns) as j:
        for c in range(4):
            beside(c, j, 0, count)
    for c in range(count - 4 * turns):
        beside(c, turns, 0, count - 4 * turns)


def wait_apart(eng, passed, *waits):
    for semaphore, value in waits:
        eng.wait_ge(semaphore, value)
    eng.sem_inc(passed, 1)


def over(ap, width):
    g = ap.shape[1]
    return ap.rearrange("p (g o) -> p g o", o=1).to_broadcast([ap.shape[0], g, width])


def norm_stats(nc, dve, t, s, b, of, g0, g1, np_=P):
    for g in range(g0, g1):
        last = nc.vector.bn_stats(t["st"][0:np_, g, :], of[0:np_, g, :])
    return last


def norm_moments(nc, dve, t, s, b, G, np_=P):
    st = t["st"][0:np_]
    dve.wait_ge(s["stats"], b.now)
    nc.vector.tensor_tensor(t["tw"][0:np_, 0:G], st[:, 0:G, 1], st[:, 0:G, 4], ALU.add)
    nc.vector.tensor_tensor(t["df"][0:np_, 0:G], st[:, 0:G, 1], st[:, 0:G, 4], ALU.subtract)
    nc.vector.tensor_tensor(t["m2"][0:np_, 0:G], st[:, 0:G, 2], st[:, 0:G, 5], ALU.add).then_inc(s["moms"], 1)
    dve.wait_ge(s["moms"], b.now)
    nc.vector.scalar_tensor_tensor(t["d2"][0:np_, 0:G], t["df"][0:np_, 0:G], 0.25, t["df"][0:np_, 0:G], ALU.mult, ALU.mult).then_inc(s["dsq"], 1)
    dve.wait_ge(s["dsq"], b.now)
    nc.vector.scalar_tensor_tensor(t["var"][0:np_, 0:G], t["m2"][0:np_, 0:G], 1.0 / F, t["d2"][0:np_, 0:G], ALU.mult, ALU.add).then_inc(s["var"], 1)


def norm_rstd(nc, act, t, s, b, G, epsc, np_=P):
    act.wait_ge(s["var"], b.now)
    nc.scalar.activation(t["ln"][0:np_, 0:G], t["var"][0:np_, 0:G], ACT.Ln, bias=epsc[0:np_, 0:1]).then_inc(s["logv"], 1)
    act.wait_ge(s["logv"], b.now)
    nc.scalar.activation(t["rs"][0:np_, 0:G], t["ln"][0:np_, 0:G], ACT.Exp, scale=-0.5).then_inc(s["rstd"], 1)


NORM_SEMS = ("stats", "moms", "dsq", "var", "logv", "rstd", "centred")


def norm_tiles(sb, G, name):
    t = {k: sb(f"{name}_{k}", [P, G]) for k in ("tw", "df", "m2", "d2", "var", "ln", "rs")}
    t["st"] = sb(f"{name}_st", [P, G, 6])
    t["ctr"] = sb(f"{name}_ctr", [P, G, F])
    return t


def gnn_kernel(nc, x, src, dst, ea, l0w1, l0b1, l0w2, l0b2, w1, b1, w2, b2, we1, be1, we2, be2,
               res_w, dot_scale, ln_g, ln_b, out):
    def dram(name, shape, dt):
        return nc.dram_tensor(name, shape, dt, kind="Internal").ap()

    agg_d = dram("agg_d", (N + P, F), fp32)
    x1_d = dram("x1_d", (N, F), fp32)
    map_d = dram("map_d", (N, 1), i32)
    src_d = dram("src_d", (EP + 2,), i32)
    dst_d = dram("dst_d", (EP + 2,), i32)
    ea_d = dram("ea_d", (EP, EF), fp32)
    eat_d = dram("eat_d", (BODIES, 2 * EF, GRP), fp32)
    flag_d = dram("flag_d", (EP,), fp32)
    st_d = dram("st_d", (2 * BODIES * P, 2 * ET * F), fp32)
    st_rows = st_d.rearrange("a (k f) -> (a k) f", f=F)
    xd_d = dram("xd_d", (BODIES * P, ET * F), fp32)

    ctx = ExitStack()
    with ctx:
        def sb(name, shape, dt=fp32):
            return ctx.enter_context(nc.sbuf_tensor(name, shape, dt))

        def pool_sem(name):
            return ctx.enter_context(nc.semaphore(name))

        ident = sb("ident", [P, P])
        cen = sb("cen", [P, P])
        avg = sb("avg", [P, P])
        ceng = sb("ceng", [P, L, P])
        cenb = sb("cenb", [P, L])
        gcol = sb("gcol", [P, L])
        bcol = sb("bcol", [P, L])
        b20 = sb("b20", [P, 1])
        onesc = sb("onesc", [P, 1])
        epsc = sb("epsc", [P, 1])
        tril = sb("tril", [P, P])
        spare = sb("spare", [P, 1])
        w10 = sb("w10", [P, HID])
        w20 = sb("w20", [P, F])
        b10 = sb("b10", [P, 1])
        wall = sb("wall", [P, L, WC])
        wcur = sb("wcur", [P, WC])
        rd = sb("rd", [P, 2, L])
        rds = sb("rds", [P, L])
        dsti = sb("dsti", [P, TILES], i32)
        srci = sb("srci", [P, TILES], i32)
        lasti = sb("lasti", [P, TILES], i32)
        srcf = sb("srcf", [P, TILES])
        rowi = sb("rowi", [P, TILES], i32)
        pidx = sb("pidx", [P, 2, TILES], i32)
        flags = sb("flags", [P, BODIES * GRP])

        PS = [ctx.enter_context(nc.psum_tensor(f"bank{i}", [P, 512], fp32)) for i in range(6)]
        PS2 = ctx.enter_context(nc.psum_tensor("banks67", [P, 1024], fp32))

        setup_edges(nc, locals())
        first_sums(nc, locals())
        first_mlp(nc, locals())
        layers(nc, locals())


@contextmanager
def semaphores(nc, prefix, clear=True):
    mine = []
    with ExitStack() as held:
        def sem(name):
            mine.append(held.enter_context(nc.semaphore(prefix + name)))
            return mine[-1]

        yield sem
        if clear:
            with nc.Block() as block:
                @block.sync
                def _(sp):
                    for k in mine:
                        sp.sem_clear(k)


def setup_edges(nc, v):
    src, dst, ea = v["src"], v["dst"], v["ea"]
    src_d, dst_d, ea_d, agg_d, map_d, st_d = (v[k] for k in ("src_d", "dst_d", "ea_d", "agg_d", "map_d", "st_d"))
    ident, cen, avg, ceng, cenb = (v[k] for k in ("ident", "cen", "avg", "ceng", "cenb"))
    gcol, bcol, wall, wcur, rd, rds = (v[k] for k in ("gcol", "bcol", "wall", "wcur", "rd", "rds"))
    flags, PS, PS2 = v["flags"], v["PS"], v["PS2"]
    AW = 12516
    CH = 1280
    with semaphores(nc, "") as sem, ExitStack() as ctx:
        def sb(name, shape, dt=fp32):
            return ctx.enter_context(nc.sbuf_tensor(name, shape, dt))

        mapfill = sb("mapfill", [CP, N // CP], i32)
        padi = sb("padi", [1, EP - E + 1], i32)
        prec = sb("prec", [1, 1], i32)
        cur = sb("cur", [HT, 2, P], i32)
        prv = sb("prv", [HT, 2, P], i32)
        gt = sb("gt", [HT, 2 * P])
        gtm = sb("gtm", [HT, 1])
        unsorted_i = sb("unsorted_i", [1, 1], i32)
        allkeys = sb("allkeys", [P, EP], i32)
        edgef = sb("edgef", [P, TILES])
        iotaf = sb("iotaf", [P, CH])
        s_key = sb("s_key", [P, 1])
        s_edge = sb("s_edge", [P, 1])
        s_lt = sb("s_lt", [P, CH])
        s_eq = sb("s_eq", [P, CH])
        s_sum = sb("s_sum", [P, 1])
        s_rank = sb("s_rank", [P, 1])
        s_ranki = sb("s_ranki", [P, 1], i32)
        s_listi = sb("s_listi", [P, 1], i32)
        s_srci = sb("s_srci", [P, 1], i32)
        s_dsti = sb("s_dsti", [P, 1], i32)
        s_ea = sb("s_ea", [P, EF])

        filled = sem("filled")
        weights_in = sem("weights_in")
        zeroed = sem("zeroed")
        padded = sem("padded")
        copied = sem("copied")
        rows_in = sem("rows_in")
        wzero = sem("wzero")
        base_made = sem("base_made")
        dchain = sem("dchain")
        over = sem("over")
        total = sem("total")
        flag_set = sem("flag_set")
        cenb_mm = sem("cenb_mm")
        cen_set = sem("cen_set")
        setup_done = sem("setup_done")
        iotas = sem("iotas")
        passed = sem("pool_passed")
        ranked = sem("ranked")
        keys_in, tile_in, moved = (v["pool_sem"](k) for k in ("keys_in", "tile_in", "moved"))

        block = ctx.enter_context(nc.Block())

        @block.sync
        def _(sp):
            sp.dma_start(dst_d[1:E + 1].rearrange("(a b) -> a b", a=8), dst.rearrange("(a b) -> a b", a=8)).then_inc(copied, 16)
            sp.dma_start(src_d[1:E + 1].rearrange("(a b) -> a b", a=8), src.rearrange("(a b) -> a b", a=8)).then_inc(copied, 16)
            sp.dma_start(ea_d[0:E, :].rearrange("(a b) f -> a (b f)", a=100), ea.rearrange("(a b) f -> a (b f)", a=100)).then_inc(copied, 16)
            sp.wait_ge(filled, 1)
            sp.dma_start(dst_d[E + 1:EP + 2].rearrange("(a b) -> a b", a=1), v_pad := padi[0:1, :]).then_inc(padded, 16)
            sp.dma_start(src_d[E + 1:EP + 2].rearrange("(a b) -> a b", a=1), v_pad).then_inc(padded, 16)
            sp.dma_start(dst_d[0:1].rearrange("(a b) -> a b", a=1), prec[:]).then_inc(padded, 16)
            sp.dma_start(src_d[0:1].rearrange("(a b) -> a b", a=1), prec[:]).then_inc(padded, 16)
            sp.wait_ge(filled, 2)
            sp.dma_start(ea_d[E:EP, :].rearrange("(a b) f -> a (b f)", a=100), flags[0:100, 0:(EP - E) // 100 * EF]).then_inc(zeroed, 16)
            sp.wait_ge(copied, 48)
            sp.wait_ge(padded, 64)
            for h in (0, 1):
                sp.dma_start(cur[:, h, :], dst_d[1 + h * EP // 2:1 + (h + 1) * EP // 2].rearrange("(q j) -> q j", j=P)).then_inc(rows_in, 16)
                sp.dma_start(prv[:, h, :], dst_d[h * EP // 2:(h + 1) * EP // 2].rearrange("(q j) -> q j", j=P)).then_inc(rows_in, 16)
            agg_v = agg_d.rearrange("a f -> (a f)").rearrange("(c p b) -> c p b", c=4, p=P)
            for c in range(4):
                sp.dma_start(agg_v[c], flags[:, 0:AW]).then_inc(zeroed, 16)
            sp.dma_start(map_d.rearrange("(p b) o -> p (b o)", p=CP), mapfill[:]).then_inc(zeroed, 16)
            st_v = st_d[BODIES * P:, :].rearrange("(c p) f -> c p f", p=P)
            for c in range(BODIES):
                sp.dma_start(st_v[c], flags[:, 0:2 * ET * F]).then_inc(zeroed, 16)
            sp.wait_ge(zeroed, 96 + 16 * BODIES)

        @block.scalar
        def _(act):
            loads = [(v["w10"][0:F, :], v["l0w1"]), (v["w10"][F:P, :], v["l0w1"]), (v["w20"][:], v["l0w2"]),
                     (v["b10"][:], v["l0b1"].rearrange("(p o) -> p o", o=1)),
                     (rd[:, 0, :], v["res_w"].rearrange("(o l) -> o l", o=1).to_broadcast([P, L])),
                     (rd[:, 1, :], v["dot_scale"].rearrange("(o l) -> o l", o=1).to_broadcast([P, L]))]
            for h in (0, 1):
                loads.append((v["b20"][h * F:(h + 1) * F, :], v["l0b2"].rearrange("(p o) -> p o", o=1)))
                for l in range(L):
                    loads.append((gcol[h * F:(h + 1) * F, l:l + 1], v["ln_g"][l].rearrange("(p o) -> p o", o=1)))
                    loads.append((bcol[h * F:(h + 1) * F, l:l + 1], v["ln_b"][l].rearrange("(p o) -> p o", o=1)))
            act.wait_ge(wzero, 1)
            for l in range(L):
                t = wall[:, l, :]
                for h in (0, 1):
                    loads.append((t[h * F:(h + 1) * F, W1_C:W1_C + HID], v["w1"][l]))
                    loads.append((t[h * EF:(h + 1) * EF, E1_C + h * F:E1_C + (h + 1) * F], v["we1"][l]))
                    loads.append((t[h * F:(h + 1) * F, E2_C + h * F:E2_C + (h + 1) * F], v["we2"][l]))
                    for c, b in ((1, v["be1"]), (2, v["b2"]), (3, v["be2"])):
                        loads.append((t[h * F:(h + 1) * F, BIAS_C + c:BIAS_C + c + 1], b[l].rearrange("(p o) -> p o", o=1)))
                loads.append((t[:, BIAS_C:BIAS_C + 1], v["b1"][l].rearrange("(p o) -> p o", o=1)))
                loads.append((t[:, W2_C:W2_C + F], v["w2"][l]))
                loads.append((t[:, G_C:G_C + F], v["ln_g"][l:l + 1, :].to_broadcast([P, F])))
                loads.append((t[:, B_C:B_C + F], v["ln_b"][l:l + 1, :].to_broadcast([P, F])))
            for to, of in loads:
                act.dma_start(to, of).then_inc(weights_in, 16)
            act.wait_ge(weights_in, 16 * len(loads))
            act.drain().then_inc(setup_done, 1)

        @block.gpsimd
        def _(pool):
            nc.gpsimd.memset(ident[:], 0.0)
            nc.gpsimd.memset(v["tril"][:], 1.0).then_inc(base_made, 1)
            pool.wait_ge(base_made, 1)
            nc.gpsimd.affine_select(out=ident[:], in_=ident[:], compare_op=ALU.not_equal, fill=1.0, base=0,
                                    pattern=[[-1, P]], channel_multiplier=1)
            nc.gpsimd.affine_select(out=v["tril"][:], in_=v["tril"][:], compare_op=ALU.is_gt, fill=0.0, base=0,
                                    pattern=[[-1, P]], channel_multiplier=1)
            nc.gpsimd.iota(v["spare"][:], pattern=[[1, 1]], base=N, channel_multiplier=1, allow_small_or_imprecise_dtypes=True)
            nc.gpsimd.iota(v["rowi"][:].rearrange("p (b t) -> p b t", t=ET), pattern=[[P * 2 * ET, BODIES], [1, ET]],
                           base=ET, channel_multiplier=2 * ET)
            nc.gpsimd.memset(v["epsc"][:], EPS)
            nc.gpsimd.memset(v["onesc"][:], 1.0).then_inc(base_made, 1)

            pool.wait_ge(flag_set, 1)
            unsorted = pool.value_load(unsorted_i[0:1, 0:1], min_val=0, max_val=P)
            with pool.If(unsorted > 0):
                pool.dma_start(allkeys[:], dst_d[1:EP + 1].rearrange("(o e) -> o e", o=1).to_broadcast([P, EP])).then_inc(keys_in, 16)
                nc.gpsimd.iota(iotaf[:], pattern=[[1, CH]], base=0, channel_multiplier=0, allow_small_or_imprecise_dtypes=True)
                nc.gpsimd.iota(edgef[:], pattern=[[P, TILES]], base=0, channel_multiplier=1,
                               allow_small_or_imprecise_dtypes=True).then_inc(iotas, 1)
                pool.wait_ge(keys_in, 16)

                def move(lo, n, np_):
                    def column(a):
                        return a[bass.ds(lo, np_)].rearrange("(p o) -> p o", o=1)

                    pool.dma_start(s_dsti[0:np_, :], column(dst)).then_inc(tile_in, 16)
                    pool.dma_start(s_srci[0:np_, :], column(src)).then_inc(tile_in, 16)
                    pool.dma_start(s_ea[0:np_, :], ea[bass.ds(lo, np_), :]).then_inc(tile_in, 16)
                    wait_apart(pool, passed, (tile_in, n * 48), (ranked, n))
                    for to, at, of in ((dst_d.rearrange("(e o) -> e o", o=1), s_listi, s_dsti),
                                       (src_d.rearrange("(e o) -> e o", o=1), s_listi, s_srci), (ea_d, s_ranki, s_ea)):
                        pool.indirect_dma_start(out=to, out_offset=bass.IndirectOffsetOnAxis(ap=at[0:np_, 0:1], axis=0),
                                                in_=of[0:np_, :], in_offset=None).then_inc(moved, 16)
                    pool.wait_ge(moved, n * 48)

                with pool.Fori(0, E // P) as t:
                    move(t * P, t + 1, P)
                move(E // P * P, E // P + 1, E % P)
            pool.nop()

        @block.vector
        def _(dve):
            chain = [0]

            def link(ins):
                chain[0] += 1
                ins.then_inc(dchain, 1)
                dve.wait_ge(dchain, chain[0])

            link(nc.vector.memset(avg[:], 0.0))
            nc.vector.memset(avg[0:F, 0:F], 1.0 / F)
            nc.vector.memset(avg[F:P, F:P], 1.0 / F)
            nc.vector.memset(padi[:], PADV)
            nc.vector.memset(prec[:], -1).then_inc(filled, 1)
            nc.vector.memset(mapfill[:], FAR)
            nc.vector.memset(flags[:], 0.0).then_inc(filled, 1)
            nc.vector.memset(wall[:], 0.0).then_inc(wzero, 1)
            dve.wait_ge(rows_in, 64)
            link(nc.vector.tensor_tensor(gt[:], prv[:].rearrange("q h j -> q (h j)"), cur[:].rearrange("q h j -> q (h j)"), ALU.is_gt))
            dve.wait_ge(base_made, 2)
            nc.vector.tensor_reduce(gtm[:], gt[:], AX.X, ALU.max).then_inc(over, 1)
            dve.wait_ge(total, 1)
            nc.vector.tensor_copy(unsorted_i[:], PS[0][0:1, 0:1]).then_inc(flag_set, 1)
            nc.vector.tensor_tensor(cen[:], ident[:], avg[:], ALU.subtract).then_inc(cen_set, 1)
            dve.wait_ge(cen_set, 1)
            dve.wait_ge(setup_done, 1)
            for l in range(L):
                nc.vector.tensor_scalar(ceng[:, l, :], cen[:], gcol[:, l:l + 1], None, ALU.mult)
            link(nc.vector.tensor_tensor(rds[:], rd[:, 0, :], rd[:, 1, :], ALU.mult))
            for l in range(L):
                nc.vector.tensor_scalar(wall[:, l, E2_C:E2_C + HID], wall[:, l, E2_C:E2_C + HID], rds[:, l:l + 1], None, ALU.mult)
                last = nc.vector.tensor_scalar(wall[:, l, BIAS_C + 3:BIAS_C + 4], wall[:, l, BIAS_C + 3:BIAS_C + 4], rds[:, l:l + 1], None, ALU.mult)
            link(last)
            nc.vector.tensor_copy(wcur[:], wall[:, 0, :])
            dve.wait_ge(cenb_mm, 1)
            link(nc.vector.tensor_copy(cenb[:], PS[1][:, 0:L]))

            dve.wait_ge(flag_set, 1)
            unsorted = dve.value_load(unsorted_i[0:1, 0:1], min_val=0, max_val=P)
            with dve.If(unsorted > 0):
                dve.wait_ge(keys_in, 16)
                dve.wait_ge(iotas, 1)

                def rank(t, n, np_):
                    dve.wait_ge(tile_in, n * 48)
                    nc.vector.tensor_copy(s_key[0:np_, :], s_dsti[0:np_, :])
                    nc.vector.tensor_copy(s_edge[:], edgef[:, bass.ds(t, 1)])
                    nc.vector.memset(s_rank[:], 0.0)
                    dve.drain()
                    with dve.Fori(0, EP // CH) as c:
                        keys = allkeys[0:np_, bass.ds(c * CH, CH)]
                        nc.vector.tensor_scalar(s_lt[0:np_, :], keys, s_key[0:np_, 0:1], None, ALU.is_lt)
                        nc.vector.tensor_scalar(s_eq[0:np_, :], keys, s_key[0:np_, 0:1], None, ALU.is_equal)
                        dve.drain()
                        nc.vector.scalar_tensor_tensor(s_eq[0:np_, :], iotaf[0:np_, :], s_edge[0:np_, 0:1], s_eq[0:np_, :],
                                                       ALU.is_lt, ALU.mult)
                        dve.drain()
                        nc.vector.tensor_tensor(s_lt[0:np_, :], s_lt[0:np_, :], s_eq[0:np_, :], ALU.add)
                        nc.vector.tensor_scalar(s_edge[:], s_edge[:], float(CH), None, ALU.subtract)
                        dve.drain()
                        nc.vector.tensor_reduce(s_sum[0:np_, :], s_lt[0:np_, :], AX.X, ALU.add)
                        dve.drain()
                        nc.vector.tensor_tensor(s_rank[0:np_, :], s_rank[0:np_, :], s_sum[0:np_, :], ALU.add)
                        dve.drain()
                    nc.vector.tensor_copy(s_ranki[:], s_rank[:])
                    nc.vector.tensor_scalar(s_listi[:], s_rank[:], 1.0, None, ALU.add).then_inc(ranked, 1)

                with dve.Fori(0, E // P) as t:
                    rank(t, t + 1, P)
                rank(E // P, E // P + 1, E % P)
            dve.nop()

        @block.tensor
        def _(pe):
            pe.wait_ge(over, 1)
            pe.wait_ge(base_made, 2)
            nc.tensor.matmul(PS[0][0:1, 0:1], gtm[:, 0:1], v["onesc"][0:HT, 0:1], start=True, stop=True).then_inc(total, 1)
            pe.wait_ge(cen_set, 1)
            pe.wait_ge(setup_done, 1)
            nc.tensor.matmul(PS[1][:, 0:L], cen[:], bcol[:], start=True, stop=True).then_inc(cenb_mm, 1)


def first_sums(nc, v):
    x, agg_d, map_d, src_d, dst_d, ea_d, eat_d, flag_d = (v[k] for k in ("x", "agg_d", "map_d", "src_d", "dst_d", "ea_d", "eat_d", "flag_d"))
    ident, tril, spare, epsc, flags = (v[k] for k in ("ident", "tril", "spare", "epsc", "flags"))
    dsti, srci, lasti, srcf, rowi, pidx = (v[k] for k in ("dsti", "srci", "lasti", "srcf", "rowi", "pidx"))
    PS = v["PS"]
    with semaphores(nc, "fs_") as sem, ExitStack() as ctx:
        def sb(name, shape, dt=fp32):
            return ctx.enter_context(nc.sbuf_tensor(name, shape, dt))

        raw = {k: sb(f"raw_{k}", [HT, 2, P], i32) for k in ("src", "cur", "prv", "nxt")}
        rowf = {k: sb(f"rowf_{k}", [HT, 2, P]) for k in ("src", "dst", "last", "eq", "flag")}
        srcbc = sb("srcbc", [P, 2, BE], i32)
        ean = sb("ean", [P, 2, ET, EF])
        eat = sb("eat", [2 * EF, 2, GRP])
        G = sb("fs_G", [P, 2, ET, F])
        H = sb("fs_H", [P, ET, F])
        eq = sb("fs_eq", [P, ET, P])
        junk = sb("fs_junk", [P, ET, P])
        sums = sb("fs_sums", [P, 2, ET, F])
        sc = sb("fs_sc", [P, ET])
        cnt = sb("fs_cnt", [P, ET])
        okm = sb("fs_okm", [P, ET])
        first = sb("fs_first", [P, ET])
        rel = sb("fs_rel", [P, ET])
        addi = sb("fs_addi", [P, 2, ET], i32)
        gi = sb("fs_gi", [P, 2, ET], i32)
        mapi = sb("fs_mapi", [P, 2, ET], i32)
        mapv = sb("fs_mapv", [P, 2, ET], i32)
        t = norm_tiles(sb, ET, "fs")

        raw_in = sem("raw_in")
        cast = sem("cast")
        dchain = sem("dchain")
        turned = sem("turned")
        lists = sem("lists")
        flags_out = sem("flags_out")
        flags_in = sem("flags_in")
        src_in = [sem("src_in0"), sem("src_in1")]
        ea_in = [sem("ea_in0"), sem("ea_in1")]
        eat_out = [sem("eat_out0"), sem("eat_out1")]
        gathered = [v["pool_sem"](f"gathered{u}") for u in (0, 1)]
        mapped = [v["pool_sem"](f"mapped{u}") for u in (0, 1)]
        one_added = [v["pool_sem"](f"one_added{k}") for k in range(ET)]
        g_clear = sem("g_clear")
        body_sems = NORM_SEMS + ("sc_set", "eqs", "cnts", "oks", "firsts", "rels", "addrs", "act_in", "selected", "summed",
                                 "ea_turned", "eat_set", "copied", "added")
        s = {k: sem(k) for k in body_sems}
        passed, pe_passed = sem("pool_passed"), sem("pe_passed")

        block = ctx.enter_context(nc.Block())
        ea_v = ea_d.rearrange("(b a k p) f -> b a k p f", a=2, k=ET // 2, p=P)

        @block.sync
        def _(sp):
            for k in body_sems:
                sp.sem_inc(s[k], CREDIT)
            for h in (0, 1):
                lo, hi = h * EP // 2, (h + 1) * EP // 2
                for k, of, o in (("src", src_d, 1), ("cur", dst_d, 1), ("prv", dst_d, 0), ("nxt", dst_d, 2)):
                    sp.dma_start(raw[k][:, h, :], of[lo + o:hi + o].rearrange("(q j) -> q j", j=P)).then_inc(raw_in, 16)
            sp.dma_start(eat_d[0], flags[0:2 * EF, 0:GRP]).then_inc(eat_out[0], 16)
            sp.wait_ge(eat_out[0], 16)
            sp.dma_start(eat_d[1], flags[0:2 * EF, 0:GRP]).then_inc(eat_out[1], 16)
            sp.wait_ge(eat_out[1], 16)
            sp.wait_ge(dchain, 3)
            sp.dma_start(flag_d.rearrange("(h q j) -> q h j", h=2, j=P), rowf["flag"][:]).then_inc(flags_out, 16)
            sp.wait_ge(flags_out, 16)
            fv = flag_d.rearrange("(o b a c) -> o a b c", o=1, a=2, c=GRP)
            for a in (0, 1):
                sp.dma_start(flags[a * F:(a + 1) * F, :].rearrange("p (b c) -> p b c", c=GRP),
                             fv[:, a, :, :].to_broadcast([F, BODIES, GRP])).then_inc(flags_in, 16)

            def load(b):
                sp.wait_ge(s["eqs"], b.older)
                sp.dma_start(srcbc[:, b.u, :], src_d[bass.ds(b.i * BE + 1, BE)].rearrange("(o e) -> o e", o=1).to_broadcast([P, BE])).then_inc(src_in[b.u], 16)
                sp.wait_ge(s["ea_turned"], b.older)
                for a in (0, 1):
                    sp.dma_start(ean[:, b.u].rearrange("p (k a) f -> p a k f", a=2)[:, a],
                                 ea_d[bass.ds(b.i * BE + a * GRP, GRP), :].rearrange("(k p) f -> p k f", p=P)).then_inc(ea_in[b.u], 16)

            staged(sp, BODIES, (1, load))
            sp.wait_ge(flags_in, 32)

        @block.gpsimd
        def _(pool):
            pool.wait_ge(lists, 1)
            pool.wait_ge(g_clear, 1)

            def ready(b):
                nc.gpsimd.tensor_copy(gi[:, b.u, :], dsti[:, bass.ds(b.i * ET, ET)])
                nc.gpsimd.tensor_copy(mapi[:, b.u, :], lasti[:, bass.ds(b.i * ET, ET)])
                nc.gpsimd.tensor_copy(mapv[:, b.u, :], rowi[:, bass.ds(b.i * ET, ET)]).then_inc(s["copied"], 1)
                wait_apart(pool, passed, (s["copied"], b.now), (s["act_in"], b.older))

            def ready_to_add(b):
                wait_apart(pool, passed, (s["addrs"], b.now), (s["summed"], b.now))

            def add_one(k):
                def step(b):
                    pool.indirect_dma_start(out=agg_d, out_offset=bass.IndirectOffsetOnAxis(ap=addi[:, b.u, k:k + 1], axis=0),
                                            in_=sums[:, b.u, k, :], in_offset=None, compute_op=ALU.add).then_inc(one_added[k], 16)
                    pool.indirect_dma_start(out=map_d, out_offset=bass.IndirectOffsetOnAxis(ap=mapi[:, b.u, k:k + 1], axis=0),
                                            in_=mapv[:, b.u, k:k + 1], in_offset=None,
                                            bounds_check=N - 1, oob_is_err=False).then_inc(mapped[b.u], 16)
                return step

            def gather_two(k):
                def step(b):
                    for kk in (2 * k, 2 * k + 1):
                        pool.indirect_dma_start(out=G[:, b.u, kk, :], out_offset=None, in_=x,
                                                in_offset=bass.IndirectOffsetOnAxis(ap=gi[:, b.u, kk:kk + 1], axis=0),
                                                bounds_check=N - 1, oob_is_err=False).then_inc(gathered[b.u], 16)
                return step

            def landed(k):
                def step(b):
                    wait_apart(pool, passed, (one_added[k], b.value("adds", (b.i + 1) * 16)))
                return step

            def all_added(b):
                pool.wait_ge(mapped[b.u], b.in2(8))
                pool.sem_inc(s["added"], 1)

            steps = [(1, ready), (0, ready_to_add)]
            for k in range(ET):
                steps += [(0, add_one(k))] + [(1, gather_two(k))] * (k < ET // 2) + [(0, landed(k))]
            staged(pool, BODIES, *steps, (0, all_added))

        @block.scalar
        def _(act):
            nc.scalar.preload_act_table_set(ACT_SET)

            def front(b):
                act.wait_ge(s["ea_turned"], b.now)
                act.wait_ge(eat_out[b.u], b.in2())
                nc.scalar.copy(eat[:, b.u, :], PS[3][0:2 * EF, 0:GRP]).then_inc(s["eat_set"], 1)
                norm_rstd(nc, act, t, s, b, ET, epsc)
                act.wait_ge(s["eat_set"], b.now)
                act.dma_start(eat_d[bass.ds(b.i, 1)].rearrange("o f c -> (o f) c"), eat[:, b.u, :]).then_inc(eat_out[b.u], 16)

            def back(b):
                act.wait_ge(s["selected"], b.now)
                act.wait_ge(s["added"], b.older)
                nc.scalar.copy(sums[:, b.u].rearrange("p k f -> p (k f)"), PS[4][:]).then_inc(s["summed"], 1)

            staged(act, BODIES, (0, back), (1, front))
            act.wait_ge(eat_out[0], 16 * ((BODIES + 1) // 2 + 1))
            act.wait_ge(eat_out[1], 16 * (BODIES // 2 + 1))

        @block.vector
        def _(dve):
            chain = [0]

            def link(ins):
                chain[0] += 1
                ins.then_inc(dchain, 1)
                dve.wait_ge(dchain, chain[0])

            nc.vector.memset(pidx[:], FAR)
            nc.vector.memset(G[:], 0.0).then_inc(g_clear, 1)
            dve.wait_ge(raw_in, 128)
            nc.vector.tensor_copy(rowf["src"][:], raw["src"][:])
            nc.vector.tensor_copy(rowf["dst"][:], raw["cur"][:])
            nc.vector.tensor_tensor(rowf["flag"][:], raw["cur"][:], raw["prv"][:], ALU.is_equal)
            link(nc.vector.tensor_tensor(rowf["eq"][:], raw["cur"][:], raw["nxt"][:], ALU.is_equal))
            link(nc.vector.scalar_tensor_tensor(rowf["last"][:], rowf["eq"][:], float(FAR), rowf["dst"][:], ALU.mult, ALU.add))
            nc.vector.memset(junk[:], 0.0).then_inc(dchain, 1)
            chain[0] += 1
            dve.wait_ge(turned, 1)
            for to, n in ((srci, 0), (srcf, 0), (dsti, 1), (lasti, 2)):
                nb = BODIES
                last = nc.vector.tensor_copy(to[:].rearrange("p (b k a) -> p b a k", b=nb, a=2),
                                             PS[n][:, 0:TILES].rearrange("p (b a k) -> p b a k", b=nb, a=2))
            last.then_inc(lists, 1)
            dve.wait_ge(lists, 1)

            def front(b):
                nc.vector.tensor_copy(sc[:], srcf[:, bass.ds(b.i * ET, ET)]).then_inc(s["sc_set"], 1)
                dve.wait_ge(s["sc_set"], b.now)
                dve.wait_ge(src_in[b.u], b.in2())
                dve.wait_ge(s["selected"], b.prev)
                for k in range(ET):
                    at = (k % 2) * GRP + (k // 2) * P
                    last = nc.vector.tensor_scalar(eq[:, k, :], srcbc[:, b.u, at:at + P], sc[:, k:k + 1], None, ALU.is_equal)
                last.then_inc(s["eqs"], 1)
                dve.wait_ge(s["eqs"], b.now)
                for k in range(ET):
                    last = nc.vector.tensor_tensor_reduce(out=junk[:, k, :], in0=eq[:, k, :], in1=tril[:], scale=1.0, scalar=0.0,
                                                          op0=ALU.mult, op1=ALU.add, accum_out=cnt[:, k:k + 1])
                last.then_inc(s["cnts"], 1)
                nc.vector.tensor_scalar(okm[:], sc[:], float(N), None, ALU.is_lt).then_inc(s["oks"], 1)
                dve.wait_ge(s["cnts"], b.now)
                dve.wait_ge(s["oks"], b.now)
                nc.vector.scalar_tensor_tensor(first[:], cnt[:], 0.5, okm[:], ALU.is_lt, ALU.mult).then_inc(s["firsts"], 1)
                dve.wait_ge(s["firsts"], b.now)
                nc.vector.scalar_tensor_tensor(rel[:], sc[:], spare[:, 0:1], first[:], ALU.subtract, ALU.mult).then_inc(s["rels"], 1)
                dve.wait_ge(s["rels"], b.now)
                dve.wait_ge(s["added"], b.older)
                nc.vector.tensor_scalar(addi[:, b.u, :], rel[:], spare[:, 0:1], None, ALU.add).then_inc(s["addrs"], 1)
                dve.wait_ge(gathered[b.u], b.in2(8))
                norm_stats(nc, dve, t, s, b, G[:, b.u], 0, ET).then_inc(s["stats"], 1)
                norm_moments(nc, dve, t, s, b, ET)
                nc.vector.scalar_tensor_tensor(t["ctr"][:], over(t["tw"][:], F), -0.5, G[:, b.u], ALU.mult, ALU.add).then_inc(s["centred"], 1)
                dve.wait_ge(s["centred"], b.now)
                dve.wait_ge(s["rstd"], b.now)
                nc.vector.scalar_tensor_tensor(H[:], t["ctr"][:], 0.0, over(t["rs"][:], F), ALU.max, ALU.mult).then_inc(s["act_in"], 1)

            staged(dve, BODIES, (1, front))

        @block.tensor
        def _(pe):
            pe.wait_ge(dchain, 2)
            for n, k in enumerate(("src", "dst", "last")):
                for h in (0, 1):
                    last = nc.tensor.transpose(PS[n][:, h * HT:(h + 1) * HT], rowf[k][:, h, :], ident[0:HT, 0:HT])
            last.then_inc(turned, 1)

            def front(b):
                wait_apart(pe, pe_passed, (ea_in[b.u], b.in2(2)), (s["eat_set"], b.prev))
                for k in range(ET // 2):
                    last = nc.tensor.transpose(PS[3][0:2 * EF, k * P:(k + 1) * P],
                                               ean[:, b.u, 2 * k:2 * k + 2, :].rearrange("p a f -> p (a f)"), ident[:])
                last.then_inc(s["ea_turned"], 1)

            def back(b):
                pe.wait_ge(s["act_in"], b.now)
                pe.wait_ge(s["summed"], b.prev)
                for k in range(ET):
                    last = nc.tensor.matmul(PS[4][:, k * F:(k + 1) * F], eq[:, k, :], H[:, k, :], start=True, stop=True)
                last.then_inc(s["selected"], 1)

            staged(pe, BODIES, (0, back), (1, front))


def first_mlp(nc, v):
    x, agg_d, map_d, x1_d = (v[k] for k in ("x", "agg_d", "map_d", "x1_d"))
    ident, epsc, w10, w20, b10, b20 = (v[k] for k in ("ident", "epsc", "w10", "w20", "b10", "b20"))
    srci, pidx, PS, PS2 = v["srci"], v["pidx"], v["PS"], v["PS2"]
    BN = P * NB
    BLK = FULL + 1
    with semaphores(nc, "fm_") as sem, ExitStack() as ctx:
        def sb(name, shape, dt=fp32):
            return ctx.enter_context(nc.sbuf_tensor(name, shape, dt))

        X = sb("fm_X", [P, 4, NB, F])
        A = sb("fm_A", [P, 4, NB, F])
        H = sb("fm_H", [P, NB, F])
        HA = sb("fm_HA", [P, NB, F])
        HT_ = sb("fm_HT", [P, NB // 2 * P])
        OT = sb("fm_OT", [P, 512])
        R = sb("fm_R", [P, 2, 512])
        Y = sb("fm_Y", [P, 2, NB, F])
        pi = sb("fm_pi", [P, 2, 2], i32)
        pv = sb("fm_pv", [P, 2, 2], i32)
        t = norm_tiles(sb, NB, "fm")

        x_in = [sem(f"x_in{w}") for w in range(4)]
        y_out = [sem("y_out0"), sem("y_out1")]
        looked = [v["pool_sem"](f"fm_looked{u}") for u in (0, 1)]
        body_sems = NORM_SEMS + ("act_in", "with_sums", "turned", "turned_set", "hidden", "hidden_set", "mlp", "out_set", "natural", "sum_set")
        s = {k: sem(k) for k in body_sems}
        looking = sem("looking")
        passed = sem("pool_passed")
        yclear = sem("yclear")

        block = ctx.enter_context(nc.Block())

        def rows(b):
            if isinstance(b.i, int) and b.i == FULL:
                return slice(FULL * BN, N), TAIL
            return bass.ds(b.i * BN, BN), P

        def nparts(b):
            return TAIL if isinstance(b.i, int) and b.i == FULL else P

        @block.sync
        def _(sp):
            for k in body_sems:
                sp.sem_inc(s[k], CREDIT)

            def load(b):
                r, n = rows(b)
                sp.wait_ge(s["sum_set"], b.oldest)
                sp.dma_start(X[0:n, b.w], x[r, :].rearrange("(p g) f -> p g f", g=NB)).then_inc(x_in[b.w], 16)
                sp.dma_start(A[0:n, b.w], agg_d[r, :].rearrange("(p g) f -> p g f", g=NB)).then_inc(x_in[b.w], 16)

            def store(b):
                r, n = rows(b)
                sp.wait_ge(s["sum_set"], b.now)
                sp.dma_start(x1_d[r, :].rearrange("(p g) f -> p g f", g=NB), Y[0:n, b.u]).then_inc(y_out[b.u], 16)

            sp.wait_ge(yclear, 1)
            for u in (0, 1):
                sp.dma_start(x1_d[u * BN:(u + 1) * BN, :].rearrange("(p g) f -> p g f", g=NB), Y[:, u]).then_inc(y_out[u], 16)
                sp.wait_ge(y_out[u], 16)
            staged(sp, BLK, (3, load), (0, store))
            sp.wait_ge(y_out[0], 16 * (BLK // 2 + 1))
            sp.wait_ge(y_out[1], 16 * (BLK // 2 + 1))

        @block.vector
        def _(dve):
            nc.vector.memset(pv[:], FAR)
            nc.vector.memset(Y[:], 0.0).then_inc(yclear, 1)

            def front(b):
                n = nparts(b)
                dve.wait_ge(x_in[b.w], b.in4(2))
                norm_stats(nc, dve, t, s, b, X[:, b.w], 0, NB, n).then_inc(s["stats"], 1)
                norm_moments(nc, dve, t, s, b, NB, n)
                nc.vector.scalar_tensor_tensor(t["ctr"][0:n], over(t["tw"][0:n], F), -0.5, X[0:n, b.w], ALU.mult, ALU.add).then_inc(s["centred"], 1)
                dve.wait_ge(s["centred"], b.now)
                dve.wait_ge(s["rstd"], b.now)
                dve.wait_ge(s["with_sums"], b.prev)
                nc.vector.scalar_tensor_tensor(H[0:n], t["ctr"][0:n], 0.0, over(t["rs"][0:n], F), ALU.max, ALU.mult).then_inc(s["act_in"], 1)

            def back(b):
                n = nparts(b)
                dve.wait_ge(s["natural"], b.now)
                dve.wait_ge(y_out[b.u], b.in2())
                nc.vector.tensor_tensor(Y[0:n, b.u].rearrange("p g f -> p (g f)"), PS[3][0:n, :],
                                        X[0:n, b.w].rearrange("p g f -> p (g f)"), ALU.add).then_inc(s["sum_set"], 1)

            staged(dve, BLK, (2, front), (0, back))

        @block.gpsimd
        def _(pool):
            pool.wait_ge(yclear, 1)

            def front(b):
                n = nparts(b)
                pool.wait_ge(s["act_in"], b.now)
                pool.wait_ge(s["turned"], b.prev)
                nc.gpsimd.tensor_tensor(HA[0:n], H[0:n], A[0:n, b.w], ALU.add).then_inc(s["with_sums"], 1)

            def look(tiles, slot, n):
                nc.gpsimd.tensor_copy(pi[:, slot, :], srci[:, tiles]).then_inc(looking, 1)
                nc.gpsimd.memset(pv[:, slot, :], FAR).then_inc(looking, 1)
                wait_apart(pool, passed, (looking, n * 3 - 1))
                for k in (0, 1):
                    pool.indirect_dma_start(out=pv[:, slot, k:k + 1], out_offset=None, in_=map_d,
                                            in_offset=bass.IndirectOffsetOnAxis(ap=pi[:, slot, k:k + 1], axis=0),
                                            bounds_check=N - 1, oob_is_err=False).then_inc(looked[slot], 16)

            def found(tiles, slot, n, uses):
                pool.wait_ge(looked[slot], uses)
                nc.gpsimd.tensor_copy(pidx[:, 0, tiles], pv[:, slot, :]).then_inc(looking, 1)
                pool.wait_ge(looking, n * 3)

            def look_b(b):
                look(bass.ds(b.i * 2, 2), b.u, b.i + 1)

            def found_b(b):
                found(bass.ds(b.i * 2, 2), b.u, b.i + 1, b.in2(2))

            staged(pool, BLK, (0, look_b), (2, front), (0, found_b))
            for i in range(BLK, TILES // 2):
                look(slice(2 * i, 2 * i + 2), i % 2, i + 1)
                found(slice(2 * i, 2 * i + 2), i % 2, i + 1, 32 * (i // 2 + 1))

        @block.scalar
        def _(act):
            nc.scalar.preload_act_table_set(ACT_SET)

            def rstd(b):
                norm_rstd(nc, act, t, s, b, NB, epsc, nparts(b))

            def turned(b):
                n = nparts(b)
                act.wait_ge(s["turned"], b.now)
                act.wait_ge(s["hidden"], b.prev)
                nc.scalar.copy(HT_[:, 0:4 * n], PS[0][:, 0:4 * n]).then_inc(s["turned_set"], 1)

            def back(b):
                n = nparts(b)
                act.wait_ge(s["hidden"], b.now)
                act.wait_ge(s["mlp"], b.prev)
                nc.scalar.activation(R[:, :, 0:4 * n], PS2[:].rearrange("p (a c) -> p a c", a=2)[:, :, 0:4 * n], ACT.Relu,
                                     bias=b10[:, 0:1]).then_inc(s["hidden_set"], 1)

            def out_turned(b):
                n = nparts(b)
                act.wait_ge(s["mlp"], b.now)
                act.wait_ge(s["natural"], b.prev)
                nc.scalar.activation(OT[:, 0:4 * n], PS[2][:, 0:4 * n], ACT.Identity, bias=b20[:, 0:1]).then_inc(s["out_set"], 1)

            staged(act, BLK, (0, back), (1, turned), (2, rstd), (0, out_turned))

        @block.tensor
        def _(pe):
            def turn(b):
                n = nparts(b)
                pe.wait_ge(s["with_sums"], b.now)
                pe.wait_ge(s["turned_set"], b.prev)
                for k in range(NB // 2):
                    last = nc.tensor.transpose(PS[0][:, k * n:(k + 1) * n],
                                               HA[0:n, 2 * k:2 * k + 2, :].rearrange("p a f -> p (a f)"), ident[0:n, 0:n])
                last.then_inc(s["turned"], 1)

            def up(b):
                n = nparts(b)
                pe.wait_ge(s["turned_set"], b.now)
                pe.wait_ge(s["hidden_set"], b.prev)
                for a in (0, 1):
                    last = nc.tensor.matmul(PS2[:, a * 512:a * 512 + 4 * n], w10[a * F:(a + 1) * F, :],
                                            HT_[a * F:(a + 1) * F, 0:4 * n], start=True, stop=True)
                last.then_inc(s["hidden"], 1)

            def back(b):
                n = nparts(b)
                pe.wait_ge(s["hidden_set"], b.now)
                pe.wait_ge(s["out_set"], b.prev)
                for a in (0, 1):
                    last = nc.tensor.matmul(PS[2][a * F:(a + 1) * F, 0:4 * n], w20[:], R[:, a, 0:4 * n], start=True, stop=True)
                last.then_inc(s["mlp"], 1)

            def turn_back(b):
                n = nparts(b)
                pe.wait_ge(s["out_set"], b.now)
                pe.wait_ge(s["sum_set"], b.prev)
                for k in range(NB // 2):
                    last = nc.tensor.transpose(PS[3][0:n, k * 2 * F:(k + 1) * 2 * F], OT[:, k * n:(k + 1) * n], ident[:])
                last.then_inc(s["natural"], 1)

            staged(pe, BLK, (1, turn), (0, back), (1, up), (0, turn_back))


def layers(nc, v):
    x1_d, map_d, st_d, st_rows, xd_d, eat_d, out = (v[k] for k in ("x1_d", "map_d", "st_d", "st_rows", "xd_d", "eat_d", "out"))
    ident, cen, avg, ceng, cenb, epsc, gcol, bcol = (v[k] for k in ("ident", "cen", "avg", "ceng", "cenb", "epsc", "gcol", "bcol"))
    wall, wcur, flags, srci, dsti, lasti, pidx = (v[k] for k in ("wall", "wcur", "flags", "srci", "dsti", "lasti", "pidx"))
    PS, PS2 = v["PS"], v["PS2"]
    NORMS = L + 1
    S2 = 2 * ET
    with semaphores(nc, "ly_", clear=False) as sem, ExitStack() as ctx:
        def sb(name, shape, dt=fp32):
            return ctx.enter_context(nc.sbuf_tensor("ly_" + name, shape, dt))

        X1 = sb("X1", [P, 4, S2, F])
        ST = sb("ST", [P, 4, S2, F])
        NS = sb("NS", [P, 2, S2, F])
        EAT = sb("EAT", [2 * EF, 4, GRP])
        XT = sb("XT", [P, GRP])
        HB = sb("HB", [P, 2, GRP])
        E1 = sb("E1", [P, GRP])
        E2 = sb("E2", [P, GRP])
        MSG = sb("MSG", [P, GRP])
        AG = sb("AG", [P, GRP])
        CAR = sb("CAR", [P, 1])
        CARB = sb("CARB", [P, 1])
        zi = sb("zi", [P, S2, F])
        gi = sb("gi", [P, 4, S2], i32)
        li = sb("li", [P, 2, ET], i32)
        XD = sb("XD", [P, 2, ET, F])
        t0 = norm_tiles(lambda n, s_, *a: sb(n, s_, *a), S2, "t0")
        t1 = norm_tiles(lambda n, s_, *a: sb(n, s_, *a), S2, "t1")
        XN = sb("XN", [P, 4, NB, F])
        YT = sb("YT", [P, CC])
        SQ = sb("SQ", [P, CC])
        LV = sb("LV", [P, CC])
        RV = sb("RV", [P, CC])
        FT = sb("FT", [P, CC])
        ON = sb("ON", [P, 2, NB, F])

        x1_in = [v["pool_sem"](f"x1_in{w}") for w in range(4)]
        xd_out = [sem(f"xd_out{w}") for w in range(4)]
        st_in = [sem(f"st_in{w}") for w in range(4)]
        looked = [v["pool_sem"](f"looked{w}") for w in range(4)]
        ea_in = [sem(f"ea_in{w}") for w in range(4)]
        st_out = [sem("st_out0"), sem("st_out1")]
        xd_in = [sem("xd_in0"), sem("xd_in1")]
        scattered = [v["pool_sem"](f"scattered{u}") for u in (0, 1)]
        xn_in = [sem(f"xn_in{w}") for w in range(4)]
        on_out = [sem("on_out0"), sem("on_out1")]
        edge_sems = ("idx", "turned", "xt", "e_up", "e1", "e1_leaky", "hidden", "hb", "hb_leaky", "e_down", "e2", "mlp", "msg", "scan_a",
                     "shift_a", "carb", "scan_b", "shift_b", "car", "back", "sum", "scaled", "gained", "done")
        s = {k: sem(k) for k in edge_sems + NORM_SEMS}
        s0 = {k: sem("first_" + k) for k in NORM_SEMS + ("ready",)}
        sl = {k: sem("last_" + k) for k in ("idx", "final", "gone")}
        node_sems = ("n_in", "n_first", "n_aff", "n_out", "n_sum")
        norm_sems = ("n_centred", "n_squared", "n_var", "n_log", "n_rstd", "n_normed")
        sn = {k: sem(k) for k in node_sems + norm_sems}
        cleared = sem("cleared")
        passed, pe_passed = sem("pool_passed"), sem("pe_passed")
        weights = sem("weights")

        block = ctx.enter_context(nc.Block())

        def state_rows(b):
            return bass.ds(((b.layer % 2) * BODIES + b.i) * P, P)

        def before_rows(b):
            return bass.ds((((b.layer + 1) % 2) * BODIES + b.i) * P, P)

        def node_rows(b):
            return bass.ds((b.layer * BODIES + b.i) * CHAIN, CHAIN)

        def all_layers(eng, begin, first, middle, last):
            staged(eng, BODIES, *first, layer=0)
            with eng.Fori(1, L - 1) as l:
                begin(l)
                staged(eng, BODIES, *middle, layer=l)
            begin(L - 1)
            staged(eng, BODIES, *last, layer=L - 1)

        @block.sync
        def _(sp):
            for k in s.values():
                sp.sem_inc(k, CREDIT)
            for k in (*s0.values(), *sl.values()):
                sp.sem_inc(k, CREDIT)
            for k in sn:
                sp.sem_inc(sn[k], CREDIT * (NORMS if k in norm_sems else 1))
            sp.wait_ge(cleared, 1)
            for w in range(4):
                sp.dma_start(xd_d[w * P:(w + 1) * P, :], X1[:, w, ET:, :].rearrange("p g f -> p (g f)")).then_inc(xd_out[w], 16)
                sp.wait_ge(xd_out[w], 16)
            for u in (0, 1):
                sp.dma_start(st_d[u * P:(u + 1) * P, :], NS[:, u].rearrange("p g f -> p (g f)")).then_inc(st_out[u], 16)
                sp.wait_ge(st_out[u], 16)
                sp.dma_start(out[u * CHAIN:(u + 1) * CHAIN, :].rearrange("(p g) f -> p g f", g=NB), ON[0:CP, u]).then_inc(on_out[u], 16)
                sp.wait_ge(on_out[u], 16)

            def load_ea(b):
                sp.wait_ge(s["e_up"], b.oldest)
                sp.dma_start(EAT[:, b.w, :], eat_d[bass.ds(b.i, 1)].rearrange("o f c -> (o f) c")).then_inc(ea_in[b.w], 16)

            def load_state(b):
                sp.wait_ge(s["centred"], b.oldest)
                sp.dma_start(ST[:, b.w].rearrange("p g f -> p (g f)"), st_d[before_rows(b), :]).then_inc(st_in[b.w], 16)

            def load_nodes(b):
                sp.wait_ge(sn["n_sum"], b.oldest)
                sp.dma_start(XN[0:CP, b.w], x1_d[node_rows(b), :].rearrange("(p g) f -> p g f", g=NB)).then_inc(xn_in[b.w], 16)

            def load_targets(b):
                sp.wait_ge(sl["gone"], b.at(2, L - 1))
                sp.dma_start(XD[:, b.u].rearrange("p g f -> p (g f)"), xd_d[bass.ds(b.i * P, P), :]).then_inc(xd_in[b.u], 16)

            def store_targets(b):
                sp.wait_ge(x1_in[b.w], b.in4(S2))
                sp.dma_start(xd_d[bass.ds(b.i * P, P), :], X1[:, b.w, ET:, :].rearrange("p g f -> p (g f)")).then_inc(xd_out[b.w], 16)

            def store_state(b):
                sp.wait_ge(s["done"], b.now)
                sp.dma_start(st_d[state_rows(b), :], NS[:, b.u].rearrange("p g f -> p (g f)")).then_inc(st_out[b.u], 16)

            def store_nodes(b):
                sp.wait_ge(sn["n_sum"], b.now)
                sp.dma_start(out[node_rows(b), :].rearrange("(p g) f -> p g f", g=NB), ON[0:CP, b.u]).then_inc(on_out[b.u], 16)

            def begin(l):
                for u in (0, 1):
                    sp.wait_ge(st_out[u], l * (16 * ((BODIES + 1 - u) // 2)) + 16)
                if isinstance(l, int):
                    for w in range(4):
                        sp.wait_ge(xd_out[w], 16 * ((BODIES + 3 - w) // 4) + 16)

            all_layers(sp, begin,
                       [(3, load_ea), (3, load_nodes), (1, store_targets), (0, store_state), (0, store_nodes)],
                       [(3, load_ea), (3, load_state), (3, load_nodes), (0, store_state), (0, store_nodes)],
                       [(3, load_ea), (3, load_state), (1, load_targets)])

        @block.gpsimd
        def _(pool):
            pool.wait_ge(cleared, 1)

            def first_idx(b):
                pool.wait_ge(s0["centred"], b.oldest)
                nc.gpsimd.tensor_copy(gi[:, b.w, 0:ET], srci[:, bass.ds(b.i * ET, ET)])
                nc.gpsimd.tensor_copy(gi[:, b.w, ET:], dsti[:, bass.ds(b.i * ET, ET)]).then_inc(s["idx"], 1)

            def gather_x1(b):
                wait_apart(pool, passed, (s["idx"], b.now), (xd_out[b.w], b.in4()))
                for k in range(S2):
                    pool.indirect_dma_start(out=X1[:, b.w, k, :], out_offset=None, in_=x1_d,
                                            in_offset=bass.IndirectOffsetOnAxis(ap=gi[:, b.w, k:k + 1], axis=0),
                                            bounds_check=N - 1, oob_is_err=False).then_inc(x1_in[b.w], 16)

            def idx(b):
                pool.wait_ge(s["turned"], b.oldest)
                nc.gpsimd.tensor_copy(gi[:, b.w, 0:ET], pidx[:, bass.ds((b.layer + 1) % 2, 1), bass.ds(b.i * ET, ET)].rearrange("p o k -> p (o k)")).then_inc(s["idx"], 1)

            def look(b):
                wait_apart(pool, passed, (s["idx"], b.now), (st_in[b.w], b.in4(skip=1)))
                for k in range(ET):
                    pool.indirect_dma_start(out=ST[:, b.w, k, :], out_offset=None, in_=st_rows,
                                            in_offset=bass.IndirectOffsetOnAxis(ap=gi[:, b.w, k:k + 1], axis=0),
                                            bounds_check=2 * ROWS - 1, oob_is_err=False).then_inc(looked[b.w], 16)

            def last_idx(b):
                nc.gpsimd.tensor_copy(li[:, b.u, :], lasti[:, bass.ds(b.i * ET, ET)]).then_inc(sl["idx"], 1)

            def scatter(b):
                wait_apart(pool, passed, (sl["idx"], b.at(0, L - 1)), (sl["final"], b.at(0, L - 1)))
                for k in range(ET):
                    pool.indirect_dma_start(out=out, out_offset=bass.IndirectOffsetOnAxis(ap=li[:, b.u, k:k + 1], axis=0),
                                            in_=XD[:, b.u, k, :], in_offset=None,
                                            bounds_check=N - 1, oob_is_err=False).then_inc(scattered[b.u], 16)
                pool.wait_ge(scattered[b.u], b.in2(ET, skip=L - 1))
                pool.sem_inc(sl["gone"], 1)

            def begin(l):
                pool.wait_ge(weights, l + 1)
                if isinstance(l, int):
                    for u in (0, 1):
                        pool.wait_ge(on_out[u], 16 * (L - 1) * ((BODIES + 1 - u) // 2) + 16)

            all_layers(pool, begin, [(2, first_idx), (2, gather_x1)], [(2, idx), (2, look)],
                       [(2, idx), (2, look), (0, last_idx), (0, scatter)])

        @block.tensor
        def _(pe):
            def turn(ready):
                def step(b):
                    pe.wait_ge(*ready(b))
                    pe.wait_ge(s["xt"], b.prev)
                    for k in range(ET // 2):
                        last = nc.tensor.transpose(PS[0][:, k * P:(k + 1) * P],
                                                   ST[:, b.w, 2 * k:2 * k + 2, :].rearrange("p a f -> p (a f)"), ident[:])
                    last.then_inc(s["turned"], 1)
                return step

            turn_first = turn(lambda b: (s0["ready"], b.now))
            turn_next = turn(lambda b: (looked[b.w], b.in4(ET, skip=1)))

            def e_up(b):
                pe.wait_ge(ea_in[b.w], b.in4())
                pe.wait_ge(s["e2"], b.prev)
                nc.tensor.matmul(PS[1][:], wcur[0:2 * EF, E1_C:E1_C + HID], EAT[:, b.w, :], start=True, stop=True).then_inc(s["e_up"], 1)

            def up(b):
                pe.wait_ge(s["xt"], b.now)
                pe.wait_ge(s["hb"], b.prev)
                for a in (0, 1):
                    last = nc.tensor.matmul(PS2[:, a * GRP:(a + 1) * GRP], wcur[a * F:(a + 1) * F, W1_C:W1_C + HID],
                                            XT[a * F:(a + 1) * F, :], start=True, stop=True)
                last.then_inc(s["hidden"], 1)

            def e_down(b):
                pe.wait_ge(s["e1_leaky"], b.now)
                nc.tensor.matmul(PS[1][:], wcur[:, E2_C:E2_C + HID], E1[:], start=True, stop=True).then_inc(s["e_down"], 1)

            def down(b):
                pe.wait_ge(s["hb_leaky"], b.now)
                pe.wait_ge(s["msg"], b.prev)
                for a in (0, 1):
                    last = nc.tensor.matmul(PS[2][a * F:(a + 1) * F, :], wcur[:, W2_C:W2_C + F], HB[:, a, :], start=True, stop=True)
                last.then_inc(s["mlp"], 1)

            def shift_a(b):
                wait_apart(pe, pe_passed, (s["scan_a"], b.now), (s["sum"], b.prev))
                nc.tensor.matmul(PS[3][F:P, 0:1], ident[0:F, 0:F], AG[0:F, GRP - 1:GRP], start=True, stop=True).then_inc(s["shift_a"], 1)

            def shift_b(b):
                wait_apart(pe, pe_passed, (s["scan_b"], b.now))
                nc.tensor.matmul(PS[3][0:F, 0:1], ident[F:P, F:P], AG[F:P, GRP - 1:GRP], start=True, stop=True).then_inc(s["shift_b"], 1)

            def turn_back(b):
                pe.wait_ge(s["car"], b.now)
                for k in range(ET // 2):
                    last = nc.tensor.transpose(PS[3][:, k * P:(k + 1) * P], AG[:, k * P:(k + 1) * P], ident[:])
                last.then_inc(s["back"], 1)

            def n_in(b):
                pe.wait_ge(xn_in[b.w], b.in4())
                pe.wait_ge(sn["n_normed"], b.part(NORMS - 1, NORMS, 1))
                for k in range(NB // 2):
                    last = nc.tensor.transpose(PS[4][:, k * CP:(k + 1) * CP],
                                               XN[0:CP, b.w, 2 * k:2 * k + 2, :].rearrange("p a f -> p (a f)"), ident[0:CP, 0:CP])
                last.then_inc(sn["n_in"], 1)

            def n_c(q):
                def step(b):
                    if q:
                        pe.wait_ge(sn["n_normed"], b.part(q - 1, NORMS))
                    else:
                        pe.wait_ge(sn["n_first"], b.now)
                    nc.tensor.matmul(PS[4][:, 0:CC], cen[:] if q < 2 else ceng[:, q - 2, :], YT[:], start=True, stop=True).then_inc(sn["n_centred"], 1)
                return step

            def n_v(q):
                def step(b):
                    pe.wait_ge(sn["n_squared"], b.part(q, NORMS))
                    if q == 0:
                        pe.wait_ge(sn["n_sum"], b.prev)
                    nc.tensor.matmul(PS[5][:, 0:CC], avg[:], SQ[:], start=True, stop=True).then_inc(sn["n_var"], 1)
                return step

            def n_out(b):
                pe.wait_ge(sn["n_aff"], b.now)
                for k in range(NB // 2):
                    last = nc.tensor.transpose(PS[5][0:CP, k * P:(k + 1) * P], FT[:, k * CP:(k + 1) * CP], ident[:])
                last.then_inc(sn["n_out"], 1)

            def begin(l):
                pe.wait_ge(weights, l + 1)

            def order(turn, nodes):
                e = [(0, down), (1, turn), (1, e_up), (0, shift_a), (1, up), (0, shift_b), (1, e_down), (0, turn_back)]
                if not nodes:
                    return e
                return [e[0], (0, n_in), e[1], (0, n_c(0)), e[2], (0, n_v(0)), e[3], (0, n_c(1)), e[4], (0, n_v(1)), e[5],
                        e[6], (0, n_c(2)), e[7], (0, n_v(2)), (0, n_c(3)), (0, n_v(3)), (0, n_c(4)), (0, n_v(4)),
                        (0, n_c(5)), (0, n_v(5)), (0, n_out)]

            all_layers(pe, begin, order(turn_first, True), order(turn_next, True), order(turn_next, False))

        @block.scalar
        def _(act):
            nc.scalar.preload_act_table_set(ACT_SET)

            def bias(c):
                return wcur[:, BIAS_C + c:BIAS_C + c + 1]

            def xt(b):
                act.wait_ge(s["turned"], b.now)
                act.wait_ge(s["hidden"], b.prev)
                nc.scalar.copy(XT[:], PS[0][:]).then_inc(s["xt"], 1)

            def e1(b):
                act.wait_ge(s["e_up"], b.now)
                act.wait_ge(s["e_down"], b.prev)
                nc.scalar.activation(E1[:], PS[1][:], ACT.Identity, bias=bias(1)).then_inc(s["e1"], 1)

            def hb(b):
                act.wait_ge(s["hidden"], b.now)
                act.wait_ge(s["mlp"], b.prev)
                nc.scalar.activation(HB[:].rearrange("p a c -> p (a c)"), PS2[:], ACT.Identity, bias=bias(0)).then_inc(s["hb"], 1)

            def e2(b):
                act.wait_ge(s["e_down"], b.now)
                act.wait_ge(s["msg"], b.prev)
                nc.scalar.activation(E2[:], PS[1][:], ACT.Identity, bias=bias(3)).then_inc(s["e2"], 1)

            def rstd0(b):
                norm_rstd(nc, act, t0, s0, b, S2, epsc)

            def rstd(G):
                return lambda b: norm_rstd(nc, act, t1, s, b, G, epsc)

            def n_first(b):
                act.wait_ge(sn["n_in"], b.now)
                nc.scalar.copy(YT[:], PS[4][:, 0:CC]).then_inc(sn["n_first"], 1)

            def n_q(q):
                def step(b):
                    act.wait_ge(sn["n_centred"], b.part(q, NORMS))
                    if q < 2:
                        nc.scalar.activation(SQ[:], PS[4][:, 0:CC], ACT.Square).then_inc(sn["n_squared"], 1)
                    else:
                        nc.scalar.activation(SQ[:], PS[4][:, 0:CC], ACT.Square, bias=cenb[:, q - 2:q - 1]).then_inc(sn["n_squared"], 1)
                return step

            def n_r(q):
                def step(b):
                    act.wait_ge(sn["n_var"], b.part(q, NORMS))
                    nc.scalar.activation(LV[:], PS[5][:, 0:CC], ACT.Ln, bias=epsc[:, 0:1]).then_inc(sn["n_log"], 1)
                    act.wait_ge(sn["n_log"], b.part(q, NORMS))
                    nc.scalar.activation(RV[:], LV[:], ACT.Exp, scale=-0.5).then_inc(sn["n_rstd"], 1)
                return step

            def n_aff(b):
                act.wait_ge(sn["n_normed"], b.part(NORMS - 1, NORMS))
                act.wait_ge(sn["n_out"], b.prev)
                nc.scalar.activation(FT[:], YT[:], ACT.Identity, bias=bcol[:, L - 1:L], scale=gcol[:, L - 1:L]).then_inc(sn["n_aff"], 1)

            def begin(l):
                act.wait_ge(weights, l + 1)

            def order(ahead, G, nodes):
                if not nodes:
                    return ahead + [(1, xt), (1, e1), (1, hb), (1, e2), (0, rstd(G))]
                return ahead + [(0, n_first), (1, xt), (0, n_q(0)), (1, e1), (0, n_r(0)), (0, n_q(1)), (1, hb), (0, n_r(1)), (1, e2),
                        (0, n_q(2)), (0, n_r(2)), (0, rstd(G)), (0, n_q(3)), (0, n_r(3)), (0, n_q(4)), (0, n_r(4)),
                        (0, n_q(5)), (0, n_r(5)), (0, n_aff)]

            all_layers(act, begin, order([(1, rstd0)], S2, True), order([], S2, True), order([], ET, False))

        @block.vector
        def _(dve):
            nc.vector.memset(X1[:], 0.0)
            nc.vector.memset(NS[:], 0.0)
            nc.vector.memset(ON[:], 0.0)
            nc.vector.memset(CAR[:], 0.0).then_inc(cleared, 1)
            nc.vector.tensor_scalar(pidx[:, 1, :], pidx[:, 0, :], float(ROWS), None, ALU.add).then_inc(weights, 1)

            def enter(b):
                dve.wait_ge(x1_in[b.w], b.in4(S2))
                norm_stats(nc, dve, t0, s0, b, X1[:, b.w], 0, S2).then_inc(s0["stats"], 1)
                norm_moments(nc, dve, t0, s0, b, S2)
                nc.vector.scalar_tensor_tensor(t0["ctr"][:], over(t0["tw"][:], F), -0.5, X1[:, b.w], ALU.mult, ALU.add).then_inc(s0["centred"], 1)

            def entered(b):
                dve.wait_ge(s0["centred"], b.now)
                dve.wait_ge(s0["rstd"], b.now)
                dve.wait_ge(s["turned"], b.older)
                nc.vector.scalar_tensor_tensor(ST[:, b.w], t0["ctr"][:], 0.0, over(t0["rs"][:], F), ALU.max, ALU.mult).then_inc(s0["ready"], 1)

            def e1_leaky(b):
                dve.wait_ge(s["e1"], b.now)
                nc.vector.scalar_tensor_tensor(E1[:], E1[:], SLOPE, E1[:], ALU.mult, ALU.max).then_inc(s["e1_leaky"], 1)

            def hb_leaky(b):
                dve.wait_ge(s["hb"], b.now)
                nc.vector.scalar_tensor_tensor(HB[:], HB[:], SLOPE, HB[:], ALU.mult, ALU.max).then_inc(s["hb_leaky"], 1)

            def msg(b):
                dve.wait_ge(s["mlp"], b.now)
                dve.wait_ge(s["e2"], b.now)
                nc.vector.scalar_tensor_tensor(MSG[:], PS[2][:], wcur[:, BIAS_C + 2:BIAS_C + 3], E2[:], ALU.add, ALU.mult).then_inc(s["msg"], 1)

            def scan_a(b):
                dve.wait_ge(s["msg"], b.now)
                dve.wait_ge(s["car"], b.prev)
                dve.wait_ge(s["back"], b.prev)
                nc.vector.tensor_tensor_scan(AG[0:F, :], flags[0:F, bass.ds(b.i * GRP, GRP)], MSG[0:F, :], CAR[0:F, 0:1],
                                             ALU.mult, ALU.add).then_inc(s["scan_a"], 1)

            def scan_b(b):
                dve.wait_ge(s["shift_a"], b.now)
                nc.vector.tensor_copy(CARB[F:P, :], PS[3][F:P, 0:1]).then_inc(s["carb"], 1)
                dve.wait_ge(s["carb"], b.now)
                nc.vector.tensor_tensor_scan(AG[F:P, :], flags[F:P, bass.ds(b.i * GRP, GRP)], MSG[F:P, :], CARB[F:P, 0:1],
                                             ALU.mult, ALU.add).then_inc(s["scan_b"], 1)

            def car(b):
                dve.wait_ge(s["shift_b"], b.now)
                nc.vector.tensor_copy(CAR[0:F, :], PS[3][0:F, 0:1]).then_inc(s["car"], 1)

            def stats_sources(ready):
                def step(b):
                    dve.wait_ge(*ready(b))
                    dve.wait_ge(s["var"], b.prev)
                    norm_stats(nc, dve, t1, s, b, ST[:, b.w], 0, ET)
                return step

            def add_sums(b):
                dve.wait_ge(s["back"], b.now)
                nc.vector.tensor_tensor(ST[:, b.w, ET:, :].rearrange("p g f -> p (g f)"), PS[3][:],
                                        ST[:, b.w, ET:, :].rearrange("p g f -> p (g f)"), ALU.add).then_inc(s["sum"], 1)

            def norm(b, lo, G, dst, slot_free):
                dve.wait_ge(s["sum"], b.now)
                for g in range(ET):
                    last = nc.vector.bn_stats(t1["st"][:, g + (ET if lo == 0 else 0), :], ST[:, b.w, ET + g, :])
                last.then_inc(s["stats"], 1)
                norm_moments(nc, dve, t1, s, b, G)
                nc.vector.scalar_tensor_tensor(t1["ctr"][:, 0:G], over(t1["tw"][:, 0:G], F), -0.5, ST[:, b.w, lo:, :], ALU.mult, ALU.add).then_inc(s["centred"], 1)
                dve.wait_ge(s["centred"], b.now)
                dve.wait_ge(s["rstd"], b.now)
                nc.vector.tensor_tensor(zi[:, 0:G], t1["ctr"][:, 0:G], over(t1["rs"][:, 0:G], F), ALU.mult).then_inc(s["scaled"], 1)

                def row(c):
                    return wcur[:, c:c + F].rearrange("p (o f) -> p o f", o=1).to_broadcast([P, G, F])

                dve.wait_ge(s["scaled"], b.now)
                nc.vector.tensor_tensor(t1["ctr"][:, 0:G], zi[:, 0:G], row(G_C), ALU.mult).then_inc(s["gained"], 1)
                dve.wait_ge(s["gained"], b.now)
                dve.wait_ge(*slot_free)
                return nc.vector.tensor_tensor(dst, t1["ctr"][:, 0:G], row(B_C), ALU.add)

            def norm_all(b):
                norm(b, 0, S2, NS[:, b.u], (st_out[b.u], b.in2())).then_inc(s["done"], 1)

            def norm_last(b):
                norm(b, ET, ET, zi[:, ET:, :], (s["gained"], b.now)).then_inc(s["done"], 1)
                dve.wait_ge(s["done"], b.now)
                dve.wait_ge(xd_in[b.u], b.in2(skip=L - 1))
                nc.vector.tensor_tensor(XD[:, b.u], XD[:, b.u], zi[:, ET:, :], ALU.add).then_inc(sl["final"], 1)

            def n_y(q):
                def step(b):
                    dve.wait_ge(sn["n_rstd"], b.part(q, NORMS))
                    if q == 0:
                        nc.vector.scalar_tensor_tensor(YT[:], PS[4][:, 0:CC], 0.0, RV[:], ALU.max, ALU.mult).then_inc(sn["n_normed"], 1)
                    else:
                        cb = 0.0 if q < 2 else cenb[:, q - 2:q - 1]
                        nc.vector.scalar_tensor_tensor(YT[:], PS[4][:, 0:CC], cb, RV[:], ALU.add, ALU.mult).then_inc(sn["n_normed"], 1)
                return step

            def n_sum(b):
                dve.wait_ge(sn["n_out"], b.now)
                dve.wait_ge(on_out[b.u], b.in2())
                nc.vector.tensor_tensor(ON[0:CP, b.u].rearrange("p g f -> p (g f)"), PS[5][0:CP, :],
                                        XN[0:CP, b.w].rearrange("p g f -> p (g f)"), ALU.add).then_inc(sn["n_sum"], 1)

            def begin(l):
                dve.wait_ge(s["done"], l * BODIES + CREDIT)
                if isinstance(l, int):
                    nc.vector.tensor_copy(wcur[:], wall[:, l, :]).then_inc(weights, 1)
                else:
                    nc.vector.tensor_copy(wcur[:], wall[:, bass.ds(l, 1), :].rearrange("p o c -> p (o c)")).then_inc(weights, 1)

            ready = lambda b: (s0["ready"], b.now)
            found = lambda b: (looked[b.w], b.in4(ET, skip=1))

            def order(ahead, src, norm_, nodes):
                e = [(0, msg), (0, scan_a)] + src + [(1, e1_leaky), (0, scan_b), (0, car), (1, hb_leaky), (0, add_sums), (0, norm_)]
                if not nodes:
                    return ahead + e
                return ahead + [(0, n_y(0)), (0, msg), (0, scan_a)] + src + [(1, e1_leaky), (0, n_y(1)), (0, scan_b), (0, car), (1, hb_leaky), (0, n_y(2)), (0, add_sums), (0, norm_),
                        (0, n_y(3)), (0, n_y(4)), (0, n_y(5)), (0, n_sum)]

            all_layers(dve, begin, order([(1, enter), (1, entered)], [(0, stats_sources(ready))], norm_all, True),
                       order([], [(0, stats_sources(found))], norm_all, True), order([], [], norm_last, False))


_INS = ['x', 'src', 'dst', 'edge_attr_32', 'L0_gnn_W1', 'L0_gnn_b1', 'L0_gnn_W2', 'L0_gnn_b2', 'L1_gnn_W1',
        'L1_gnn_b1', 'L1_gnn_W2', 'L1_gnn_b2', 'L1_gnn_We1', 'L1_gnn_be1', 'L1_gnn_We2', 'L1_gnn_be2',
        'L1_gnn_res_w', 'L1_gnn_dot_scale', 'L1_gnn_ln_g', 'L1_gnn_ln_b']
_OUTS = [((100000, 64), 'float32')]


def kernel(**inputs):
    import numpy as _np
    import concourse.bacc as _bacc
    from concourse import mybir as _mybir
    from concourse.bass_utils import run_bass_kernel_spmd as _run

    nc = _bacc.Bacc("TRN2", target_bir_lowering=False, num_devices=1)
    arrays, args = {}, []
    for name in _INS:
        a = _np.ascontiguousarray(inputs[name])
        arrays[f"in_{name}_dram"] = a
        args.append(nc.dram_tensor(f"in_{name}_dram", a.shape, _mybir.dt.from_np(a.dtype), kind="ExternalInput").ap())
    for i, (shape, dtype) in enumerate(_OUTS):
        dt = _mybir.dt.from_np(_np.dtype(dtype))
        args.append(nc.dram_tensor(f"out_{i}_dram", shape, dt, kind="ExternalOutput").ap())
    gnn_kernel(nc, *args)
    r = _run(nc, [arrays], core_ids=[0])
    got = tuple(r.results[0][f"out_{i}_dram"] for i in range(len(_OUTS)))
    return got[0]
```

```python
import concourse.bass as bass
from concourse import mybir
from contextlib import ExitStack, contextmanager

fp32 = mybir.dt.float32
i32 = mybir.dt.int32
ALU = mybir.AluOpType
ACT = mybir.ActivationFunctionType
AX = mybir.AxisListType

N = 100000
E = 25000
F = 64
HID = 128
EF = 32
L = 5
EPS = 1e-5
ACT_SET = "natural_log_exp_and_others"
SLOPE = 0.1

P = 128
ET = 8
BE = ET * P
BODIES = -(-E // BE)
EP = BODIES * BE
GRP = BE // 2
TILES = EP // P
HT = TILES // 2
PADV = 131071
FAR = 1 << 20
ROWS = BODIES * P * 2 * ET

NB = 8
FULL = N // (P * NB)
TAIL = (N - FULL * P * NB) // NB
CP = 125
CHAIN = CP * NB
CC = CHAIN // 2

W1_C, W2_C, E1_C, E2_C, G_C, B_C, BIAS_C = 0, 128, 192, 320, 448, 512, 576
WC = BIAS_C + 4


CREDIT = 4


class Body:

    def __init__(self, eng, c, j, count, layer):
        self.eng, self.i, self.u, self.w, self.known = eng, j * 4 + c, c % 2, c % 4, {}
        self.c, self.j, self.count, self.layer = c, j, count, layer

    def value(self, key, x):
        if key not in self.known:
            self.known[key] = x if isinstance(x, int) else self.eng.snap(x)
        return self.known[key]

    def at(self, back, skip=0):
        return self.value(("at", back, skip), (self.layer - skip) * self.count + self.i + 1 + CREDIT - back)

    now = property(lambda self: self.at(0))
    prev = property(lambda self: self.at(1))
    older = property(lambda self: self.at(2))
    oldest = property(lambda self: self.at(4))

    def of(self, d):
        if isinstance(self.i, int):
            d = min(d, self.count - 1 - self.i)
        return self.at(-d)

    def in2(self, m=1, more=0, skip=0):
        uses = (self.layer - skip) * ((self.count + 1 - self.u) // 2) + self.j * 2 + self.c // 2 + 1
        return self.value(("in2", m, more, skip), uses * (16 * m) + 16 * more)

    def in4(self, m=1, more=0, skip=0):
        uses = (self.layer - skip) * ((self.count + 3 - self.w) // 4) + self.j + self.c // 4 + 1
        return self.value(("in4", m, more, skip), uses * (16 * m) + 16 * more)


def staged(eng, count, *stages, layer=0):
    top = max(ahead for ahead, _ in stages)

    def beside(c, j, lo, hi):
        bodies = {}
        for ahead, step in stages:
            if lo <= c + ahead < hi:
                if ahead not in bodies:
                    bodies[ahead] = Body(eng, c + ahead, j, count, layer)
                step(bodies[ahead])

    turns = (count - top) // 4
    for c in range(-top, 0):
        beside(c, 0, 0, count)
    with eng.Fori(0, turns) as j:
        for c in range(4):
            beside(c, j, 0, count)
    for c in range(count - 4 * turns):
        beside(c, turns, 0, count - 4 * turns)


def wait_apart(eng, passed, *waits):
    for semaphore, value in waits:
        eng.wait_ge(semaphore, value)
    eng.sem_inc(passed, 1)


def over(ap, width):
    g = ap.shape[1]
    return ap.rearrange("p (g o) -> p g o", o=1).to_broadcast([ap.shape[0], g, width])


def norm_stats(nc, dve, t, s, b, of, g0, g1, np_=P):
    for g in range(g0, g1):
        last = nc.vector.bn_stats(t["st"][0:np_, g, :], of[0:np_, g, :])
    return last


def norm_moments(nc, dve, t, s, b, G, np_=P):
    st = t["st"][0:np_]
    dve.wait_ge(s["stats"], b.now)
    nc.vector.tensor_tensor(t["tw"][0:np_, 0:G], st[:, 0:G, 1], st[:, 0:G, 4], ALU.add)
    nc.vector.tensor_tensor(t["df"][0:np_, 0:G], st[:, 0:G, 1], st[:, 0:G, 4], ALU.subtract)
    nc.vector.tensor_tensor(t["m2"][0:np_, 0:G], st[:, 0:G, 2], st[:, 0:G, 5], ALU.add).then_inc(s["moms"], 1)
    dve.wait_ge(s["moms"], b.now)
    nc.vector.scalar_tensor_tensor(t["d2"][0:np_, 0:G], t["df"][0:np_, 0:G], 0.25, t["df"][0:np_, 0:G], ALU.mult, ALU.mult).then_inc(s["dsq"], 1)
    dve.wait_ge(s["dsq"], b.now)
    nc.vector.scalar_tensor_tensor(t["var"][0:np_, 0:G], t["m2"][0:np_, 0:G], 1.0 / F, t["d2"][0:np_, 0:G], ALU.mult, ALU.add).then_inc(s["var"], 1)


def norm_rstd(nc, act, t, s, b, G, epsc, np_=P):
    act.wait_ge(s["var"], b.now)
    nc.scalar.activation(t["ln"][0:np_, 0:G], t["var"][0:np_, 0:G], ACT.Ln, bias=epsc[0:np_, 0:1]).then_inc(s["logv"], 1)
    act.wait_ge(s["logv"], b.now)
    nc.scalar.activation(t["rs"][0:np_, 0:G], t["ln"][0:np_, 0:G], ACT.Exp, scale=-0.5).then_inc(s["rstd"], 1)


NORM_SEMS = ("stats", "moms", "dsq", "var", "logv", "rstd", "centred")


def norm_tiles(sb, G, name):
    t = {k: sb(f"{name}_{k}", [P, G]) for k in ("tw", "df", "m2", "d2", "var", "ln", "rs")}
    t["st"] = sb(f"{name}_st", [P, G, 6])
    t["ctr"] = sb(f"{name}_ctr", [P, G, F])
    return t


def gnn_kernel(nc, x, src, dst, ea, l0w1, l0b1, l0w2, l0b2, w1, b1, w2, b2, we1, be1, we2, be2,
               res_w, dot_scale, ln_g, ln_b, out):
    def dram(name, shape, dt):
        return nc.dram_tensor(name, shape, dt, kind="Internal").ap()

    agg_d = dram("agg_d", (N + P, F), fp32)
    x1_d = dram("x1_d", (N, F), fp32)
    map_d = dram("map_d", (N, 1), i32)
    src_d = dram("src_d", (EP + 2,), i32)
    dst_d = dram("dst_d", (EP + 2,), i32)
    ea_d = dram("ea_d", (EP, EF), fp32)
    eat_d = dram("eat_d", (BODIES, 2 * EF, GRP), fp32)
    flag_d = dram("flag_d", (EP,), fp32)
    st_d = dram("st_d", (2 * BODIES * P, 2 * ET * F), fp32)
    st_rows = st_d.rearrange("a (k f) -> (a k) f", f=F)
    xd_d = dram("xd_d", (BODIES * P, ET * F), fp32)

    ctx = ExitStack()
    with ctx:
        def sb(name, shape, dt=fp32):
            return ctx.enter_context(nc.sbuf_tensor(name, shape, dt))

        def pool_sem(name):
            return ctx.enter_context(nc.semaphore(name))

        ident = sb("ident", [P, P])
        cen = sb("cen", [P, P])
        avg = sb("avg", [P, P])
        ceng = sb("ceng", [P, L, P])
        cenb = sb("cenb", [P, L])
        gcol = sb("gcol", [P, L])
        bcol = sb("bcol", [P, L])
        b20 = sb("b20", [P, 1])
        onesc = sb("onesc", [P, 1])
        epsc = sb("epsc", [P, 1])
        tril = sb("tril", [P, P])
        spare = sb("spare", [P, 1])
        w10 = sb("w10", [P, HID])
        w20 = sb("w20", [P, F])
        b10 = sb("b10", [P, 1])
        wall = sb("wall", [P, L, WC])
        wcur = sb("wcur", [P, WC])
        rd = sb("rd", [P, 2, L])
        rds = sb("rds", [P, L])
        dsti = sb("dsti", [P, TILES], i32)
        srci = sb("srci", [P, TILES], i32)
        lasti = sb("lasti", [P, TILES], i32)
        srcf = sb("srcf", [P, TILES])
        rowi = sb("rowi", [P, TILES], i32)
        pidx = sb("pidx", [P, 2, TILES], i32)
        flags = sb("flags", [P, BODIES * GRP])

        PS = [ctx.enter_context(nc.psum_tensor(f"bank{i}", [P, 512], fp32)) for i in range(6)]
        PS2 = ctx.enter_context(nc.psum_tensor("banks67", [P, 1024], fp32))

        agg_zeroed = pool_sem("agg_zeroed")
        CLEARS = 16
        setup_edges(nc, locals())
        first_sums(nc, locals())
        first_mlp(nc, locals())
        layers(nc, locals())


@contextmanager
def semaphores(nc, prefix, clear=True):
    mine = []
    with ExitStack() as held:
        def sem(name):
            mine.append(held.enter_context(nc.semaphore(prefix + name)))
            return mine[-1]

        yield sem
        if clear:
            with nc.Block() as block:
                @block.sync
                def _(sp):
                    for k in mine:
                        sp.sem_clear(k)


def setup_edges(nc, v):
    src, dst, ea = v["src"], v["dst"], v["ea"]
    src_d, dst_d, ea_d, agg_d, map_d = (v[k] for k in ("src_d", "dst_d", "ea_d", "agg_d", "map_d"))
    ident, cen, avg, ceng, cenb = (v[k] for k in ("ident", "cen", "avg", "ceng", "cenb"))
    gcol, bcol, wall, wcur, rd, rds = (v[k] for k in ("gcol", "bcol", "wall", "wcur", "rd", "rds"))
    flags, PS, PS2 = v["flags"], v["PS"], v["PS2"]
    CH = 1280
    with semaphores(nc, "") as sem, ExitStack() as ctx:
        def sb(name, shape, dt=fp32):
            return ctx.enter_context(nc.sbuf_tensor(name, shape, dt))

        mapfill = sb("mapfill", [CP, N // CP], i32)
        padi = sb("padi", [1, EP - E + 1], i32)
        prec = sb("prec", [1, 1], i32)
        cur = sb("cur", [HT, 2, P], i32)
        prv = sb("prv", [HT, 2, P], i32)
        gt = sb("gt", [HT, 2 * P])
        gtm = sb("gtm", [HT, 1])
        unsorted_i = sb("unsorted_i", [1, 1], i32)
        allkeys = sb("allkeys", [P, EP], i32)
        edgef = sb("edgef", [P, TILES])
        iotaf = sb("iotaf", [P, CH])
        s_key = sb("s_key", [P, 1])
        s_edge = sb("s_edge", [P, 1])
        s_lt = sb("s_lt", [P, CH])
        s_eq = sb("s_eq", [P, CH])
        s_sum = sb("s_sum", [P, 1])
        s_rank = sb("s_rank", [P, 1])
        s_ranki = sb("s_ranki", [P, 1], i32)
        s_listi = sb("s_listi", [P, 1], i32)
        s_srci = sb("s_srci", [P, 1], i32)
        s_dsti = sb("s_dsti", [P, 1], i32)
        s_ea = sb("s_ea", [P, EF])

        filled = sem("filled")
        zeroed = sem("zeroed")
        padded = sem("padded")
        copied = sem("copied")
        rows_in = sem("rows_in")
        base_made = sem("base_made")
        dchain = sem("dchain")
        over = sem("over")
        total = sem("total")
        flag_set = sem("flag_set")
        iotas = sem("iotas")
        passed = sem("pool_passed")
        ranked = sem("ranked")
        keys_in, tile_in, moved = (v["pool_sem"](k) for k in ("keys_in", "tile_in", "moved"))

        block = ctx.enter_context(nc.Block())

        @block.sync
        def _(sp):
            sp.dma_start(dst_d[1:E + 1].rearrange("(a b) -> a b", a=8), dst.rearrange("(a b) -> a b", a=8)).then_inc(copied, 16)
            sp.dma_start(src_d[1:E + 1].rearrange("(a b) -> a b", a=8), src.rearrange("(a b) -> a b", a=8)).then_inc(copied, 16)
            sp.dma_start(ea_d[0:E, :].rearrange("(a b) f -> a (b f)", a=100), ea.rearrange("(a b) f -> a (b f)", a=100)).then_inc(copied, 16)
            sp.wait_ge(filled, 1)
            sp.dma_start(dst_d[E + 1:EP + 2].rearrange("(a b) -> a b", a=1), v_pad := padi[0:1, :]).then_inc(padded, 16)
            sp.dma_start(src_d[E + 1:EP + 2].rearrange("(a b) -> a b", a=1), v_pad).then_inc(padded, 16)
            sp.dma_start(dst_d[0:1].rearrange("(a b) -> a b", a=1), prec[:]).then_inc(padded, 16)
            sp.dma_start(src_d[0:1].rearrange("(a b) -> a b", a=1), prec[:]).then_inc(padded, 16)
            sp.wait_ge(filled, 2)
            sp.dma_start(ea_d[E:EP, :].rearrange("(a b) f -> a (b f)", a=100), flags[0:100, 0:(EP - E) // 100 * EF]).then_inc(zeroed, 16)
            sp.wait_ge(copied, 48)
            sp.wait_ge(padded, 64)
            agg_v = agg_d.rearrange("a f -> (a f)").rearrange("(c p b) -> c p b", c=v["CLEARS"], p=P)
            for h in (0, 1):
                sp.dma_start(cur[:, h, :], dst_d[1 + h * EP // 2:1 + (h + 1) * EP // 2].rearrange("(q j) -> q j", j=P)).then_inc(rows_in, 16)
                sp.dma_start(prv[:, h, :], dst_d[h * EP // 2:(h + 1) * EP // 2].rearrange("(q j) -> q j", j=P)).then_inc(rows_in, 16)
            sp.dma_start(map_d.rearrange("(p b) o -> p (b o)", p=CP), mapfill[:]).then_inc(zeroed, 16)
            for c in range(v["CLEARS"]):
                sp.dma_start(agg_v[c], flags[:, 0:agg_v.shape[2]]).then_inc(v["agg_zeroed"], 16)
            sp.wait_ge(zeroed, 32)

        @block.gpsimd
        def _(pool):
            nc.gpsimd.memset(ident[:], 0.0)
            nc.gpsimd.memset(v["tril"][:], 1.0).then_inc(base_made, 1)
            pool.wait_ge(base_made, 1)
            nc.gpsimd.affine_select(out=ident[:], in_=ident[:], compare_op=ALU.not_equal, fill=1.0, base=0,
                                    pattern=[[-1, P]], channel_multiplier=1)
            nc.gpsimd.affine_select(out=v["tril"][:], in_=v["tril"][:], compare_op=ALU.is_gt, fill=0.0, base=0,
                                    pattern=[[-1, P]], channel_multiplier=1)
            nc.gpsimd.iota(v["spare"][:], pattern=[[1, 1]], base=N, channel_multiplier=1, allow_small_or_imprecise_dtypes=True)
            nc.gpsimd.iota(v["rowi"][:].rearrange("p (b t) -> p b t", t=ET), pattern=[[P * 2 * ET, BODIES], [1, ET]],
                           base=ET, channel_multiplier=2 * ET)
            nc.gpsimd.memset(v["epsc"][:], EPS)
            nc.gpsimd.memset(v["onesc"][:], 1.0).then_inc(base_made, 1)

            pool.wait_ge(flag_set, 1)
            unsorted = pool.value_load(unsorted_i[0:1, 0:1], min_val=0, max_val=P)
            with pool.If(unsorted > 0):
                pool.dma_start(allkeys[:], dst_d[1:EP + 1].rearrange("(o e) -> o e", o=1).to_broadcast([P, EP])).then_inc(keys_in, 16)
                nc.gpsimd.iota(iotaf[:], pattern=[[1, CH]], base=0, channel_multiplier=0, allow_small_or_imprecise_dtypes=True)
                nc.gpsimd.iota(edgef[:], pattern=[[P, TILES]], base=0, channel_multiplier=1,
                               allow_small_or_imprecise_dtypes=True).then_inc(iotas, 1)
                pool.wait_ge(keys_in, 16)

                def move(lo, n, np_):
                    def column(a):
                        return a[bass.ds(lo, np_)].rearrange("(p o) -> p o", o=1)

                    pool.dma_start(s_dsti[0:np_, :], column(dst)).then_inc(tile_in, 16)
                    pool.dma_start(s_srci[0:np_, :], column(src)).then_inc(tile_in, 16)
                    pool.dma_start(s_ea[0:np_, :], ea[bass.ds(lo, np_), :]).then_inc(tile_in, 16)
                    wait_apart(pool, passed, (tile_in, n * 48), (ranked, n))
                    for to, at, of in ((dst_d.rearrange("(e o) -> e o", o=1), s_listi, s_dsti),
                                       (src_d.rearrange("(e o) -> e o", o=1), s_listi, s_srci), (ea_d, s_ranki, s_ea)):
                        pool.indirect_dma_start(out=to, out_offset=bass.IndirectOffsetOnAxis(ap=at[0:np_, 0:1], axis=0),
                                                in_=of[0:np_, :], in_offset=None).then_inc(moved, 16)
                    pool.wait_ge(moved, n * 48)

                with pool.Fori(0, E // P) as t:
                    move(t * P, t + 1, P)
                move(E // P * P, E // P + 1, E % P)
            pool.nop()

        @block.vector
        def _(dve):
            chain = [0]

            def link(ins):
                chain[0] += 1
                ins.then_inc(dchain, 1)
                dve.wait_ge(dchain, chain[0])

            link(nc.vector.memset(avg[:], 0.0))
            nc.vector.memset(avg[0:F, 0:F], 1.0 / F)
            nc.vector.memset(avg[F:P, F:P], 1.0 / F)
            nc.vector.memset(padi[:], PADV)
            nc.vector.memset(prec[:], -1).then_inc(filled, 1)
            nc.vector.memset(mapfill[:], FAR)
            nc.vector.memset(flags[:], 0.0).then_inc(filled, 1)
            link(nc.vector.memset(wall[:], 0.0))
            dve.wait_ge(base_made, 2)
            link(nc.vector.tensor_tensor(cen[:], ident[:], avg[:], ALU.subtract))
            dve.wait_ge(rows_in, 64)
            link(nc.vector.tensor_tensor(gt[:], prv[:].rearrange("q h j -> q (h j)"), cur[:].rearrange("q h j -> q (h j)"), ALU.is_gt))
            nc.vector.tensor_reduce(gtm[:], gt[:], AX.X, ALU.max).then_inc(over, 1)
            dve.wait_ge(total, 1)
            nc.vector.tensor_copy(unsorted_i[:], PS[0][0:1, 0:1]).then_inc(flag_set, 1)
            dve.wait_ge(flag_set, 1)
            unsorted = dve.value_load(unsorted_i[0:1, 0:1], min_val=0, max_val=P)
            with dve.If(unsorted > 0):
                dve.wait_ge(keys_in, 16)
                dve.wait_ge(iotas, 1)

                def rank(t, n, np_):
                    dve.wait_ge(tile_in, n * 48)
                    nc.vector.tensor_copy(s_key[0:np_, :], s_dsti[0:np_, :])
                    nc.vector.tensor_copy(s_edge[:], edgef[:, bass.ds(t, 1)])
                    nc.vector.memset(s_rank[:], 0.0)
                    dve.drain()
                    with dve.Fori(0, EP // CH) as c:
                        keys = allkeys[0:np_, bass.ds(c * CH, CH)]
                        nc.vector.tensor_scalar(s_lt[0:np_, :], keys, s_key[0:np_, 0:1], None, ALU.is_lt)
                        nc.vector.tensor_scalar(s_eq[0:np_, :], keys, s_key[0:np_, 0:1], None, ALU.is_equal)
                        dve.drain()
                        nc.vector.scalar_tensor_tensor(s_eq[0:np_, :], iotaf[0:np_, :], s_edge[0:np_, 0:1], s_eq[0:np_, :],
                                                       ALU.is_lt, ALU.mult)
                        dve.drain()
                        nc.vector.tensor_tensor(s_lt[0:np_, :], s_lt[0:np_, :], s_eq[0:np_, :], ALU.add)
                        nc.vector.tensor_scalar(s_edge[:], s_edge[:], float(CH), None, ALU.subtract)
                        dve.drain()
                        nc.vector.tensor_reduce(s_sum[0:np_, :], s_lt[0:np_, :], AX.X, ALU.add)
                        dve.drain()
                        nc.vector.tensor_tensor(s_rank[0:np_, :], s_rank[0:np_, :], s_sum[0:np_, :], ALU.add)
                        dve.drain()
                    nc.vector.tensor_copy(s_ranki[:], s_rank[:])
                    nc.vector.tensor_scalar(s_listi[:], s_rank[:], 1.0, None, ALU.add).then_inc(ranked, 1)

                with dve.Fori(0, E // P) as t:
                    rank(t, t + 1, P)
                rank(E // P, E // P + 1, E % P)
            dve.nop()

        @block.tensor
        def _(pe):
            pe.wait_ge(over, 1)
            pe.wait_ge(base_made, 2)
            nc.tensor.matmul(PS[0][0:1, 0:1], gtm[:, 0:1], v["onesc"][0:HT, 0:1], start=True, stop=True).then_inc(total, 1)


def load_weights(act, v, weights_in):
    rd, gcol, bcol, wall = (v[k] for k in ("rd", "gcol", "bcol", "wall"))
    loads = [(v["w10"][0:F, :], v["l0w1"]), (v["w10"][F:P, :], v["l0w1"]), (v["w20"][:], v["l0w2"]),
             (v["b10"][:], v["l0b1"].rearrange("(p o) -> p o", o=1)),
             (rd[:, 0, :], v["res_w"].rearrange("(o l) -> o l", o=1).to_broadcast([P, L])),
             (rd[:, 1, :], v["dot_scale"].rearrange("(o l) -> o l", o=1).to_broadcast([P, L]))]
    for h in (0, 1):
        loads.append((v["b20"][h * F:(h + 1) * F, :], v["l0b2"].rearrange("(p o) -> p o", o=1)))
        for l in range(L):
            loads.append((gcol[h * F:(h + 1) * F, l:l + 1], v["ln_g"][l].rearrange("(p o) -> p o", o=1)))
            loads.append((bcol[h * F:(h + 1) * F, l:l + 1], v["ln_b"][l].rearrange("(p o) -> p o", o=1)))
    for l in range(L):
        t = wall[:, l, :]
        for h in (0, 1):
            loads.append((t[h * F:(h + 1) * F, W1_C:W1_C + HID], v["w1"][l]))
            loads.append((t[h * EF:(h + 1) * EF, E1_C + h * F:E1_C + (h + 1) * F], v["we1"][l]))
            loads.append((t[h * F:(h + 1) * F, E2_C + h * F:E2_C + (h + 1) * F], v["we2"][l]))
            for c, b in ((1, v["be1"]), (2, v["b2"]), (3, v["be2"])):
                loads.append((t[h * F:(h + 1) * F, BIAS_C + c:BIAS_C + c + 1], b[l].rearrange("(p o) -> p o", o=1)))
        loads.append((t[:, BIAS_C:BIAS_C + 1], v["b1"][l].rearrange("(p o) -> p o", o=1)))
        loads.append((t[:, W2_C:W2_C + F], v["w2"][l]))
        loads.append((t[:, G_C:G_C + F], v["ln_g"][l:l + 1, :].to_broadcast([P, F])))
        loads.append((t[:, B_C:B_C + F], v["ln_b"][l:l + 1, :].to_broadcast([P, F])))
    for to, of in loads:
        act.dma_start(to, of).then_inc(weights_in, 16)
    return len(loads)


def first_sums(nc, v):
    x, agg_d, src_d, dst_d, ea_d, eat_d, flag_d = (v[k] for k in ("x", "agg_d", "src_d", "dst_d", "ea_d", "eat_d", "flag_d"))
    ident, tril, spare, epsc, flags = (v[k] for k in ("ident", "tril", "spare", "epsc", "flags"))
    cen, ceng, cenb, gcol, bcol, wall, wcur, rd, rds = (v[k] for k in ("cen", "ceng", "cenb", "gcol", "bcol", "wall", "wcur", "rd", "rds"))
    dsti, srci, lasti, srcf = (v[k] for k in ("dsti", "srci", "lasti", "srcf"))
    PS = v["PS"]
    agg_zeroed = v["agg_zeroed"]
    CLEARS = v["CLEARS"]
    LOADS = 8 + 4 * L + L * (2 * 6 + 4)
    with semaphores(nc, "fs_") as sem, ExitStack() as ctx:
        def sb(name, shape, dt=fp32):
            return ctx.enter_context(nc.sbuf_tensor(name, shape, dt))

        raw = {k: sb(f"raw_{k}", [HT, 2, P], i32) for k in ("src", "cur", "prv", "nxt")}
        rowf = {k: sb(f"rowf_{k}", [HT, 2, P]) for k in ("src", "dst", "last", "eq", "flag")}
        srcbc = sb("srcbc", [P, 2, BE], i32)
        ean = sb("ean", [P, 2, ET, EF])
        eat = sb("eat", [2 * EF, 2, GRP])
        G = sb("fs_G", [P, 2, ET, F])
        H = sb("fs_H", [P, ET, F])
        eq = sb("fs_eq", [P, ET, P])
        junk = sb("fs_junk", [P, ET, P])
        sums = sb("fs_sums", [P, 2, ET, F])
        sc = sb("fs_sc", [P, ET])
        cnt = sb("fs_cnt", [P, ET])
        okm = sb("fs_okm", [P, ET])
        first = sb("fs_first", [P, ET])
        rel = sb("fs_rel", [P, ET])
        addi = sb("fs_addi", [P, 2, ET], i32)
        gi = sb("fs_gi", [P, 2, ET], i32)
        t = norm_tiles(sb, ET, "fs")

        raw_in = sem("raw_in")
        dchain = sem("dchain")
        turned = sem("turned")
        lists = sem("lists")
        weights_in = sem("weights_in")
        cenb_mm = sem("cenb_mm")
        flags_out = sem("flags_out")
        flags_in = sem("flags_in")
        src_in = [sem("src_in0"), sem("src_in1")]
        ea_in = [sem("ea_in0"), sem("ea_in1")]
        eat_out = [sem("eat_out0"), sem("eat_out1")]
        gathered = [v["pool_sem"](f"gathered{u}") for u in (0, 1)]
        one_added = [v["pool_sem"](f"one_added{k}") for k in range(ET)]
        g_clear = sem("g_clear")
        body_sems = NORM_SEMS + ("sc_set", "eqs", "cnts", "oks", "firsts", "rels", "addrs", "act_in", "selected", "summed",
                                 "ea_turned", "eat_set", "copied", "added")
        s = {k: sem(k) for k in body_sems}
        passed, pe_passed = sem("pool_passed"), sem("pe_passed")

        block = ctx.enter_context(nc.Block())
        ea_v = ea_d.rearrange("(b a k p) f -> b a k p f", a=2, k=ET // 2, p=P)

        @block.sync
        def _(sp):
            for k in body_sems:
                sp.sem_inc(s[k], CREDIT)
            for h in (0, 1):
                lo, hi = h * EP // 2, (h + 1) * EP // 2
                for k, of, o in (("src", src_d, 1), ("cur", dst_d, 1), ("prv", dst_d, 0), ("nxt", dst_d, 2)):
                    sp.dma_start(raw[k][:, h, :], of[lo + o:hi + o].rearrange("(q j) -> q j", j=P)).then_inc(raw_in, 16)
            sp.dma_start(eat_d[0], flags[0:2 * EF, 0:GRP]).then_inc(eat_out[0], 16)
            sp.wait_ge(eat_out[0], 16)
            sp.dma_start(eat_d[1], flags[0:2 * EF, 0:GRP]).then_inc(eat_out[1], 16)
            sp.wait_ge(eat_out[1], 16)
            sp.wait_ge(dchain, 3)
            sp.dma_start(flag_d.rearrange("(h q j) -> q h j", h=2, j=P), rowf["flag"][:]).then_inc(flags_out, 16)
            sp.wait_ge(flags_out, 16)
            sp.wait_ge(agg_zeroed, 16 * CLEARS)
            fv = flag_d.rearrange("(o b a c) -> o a b c", o=1, a=2, c=GRP)
            for a in (0, 1):
                sp.dma_start(flags[a * F:(a + 1) * F, :].rearrange("p (b c) -> p b c", c=GRP),
                             fv[:, a, :, :].to_broadcast([F, BODIES, GRP])).then_inc(flags_in, 16)

            def load(b):
                sp.wait_ge(s["eqs"], b.older)
                sp.dma_start(srcbc[:, b.u, :], src_d[bass.ds(b.i * BE + 1, BE)].rearrange("(o e) -> o e", o=1).to_broadcast([P, BE])).then_inc(src_in[b.u], 16)
                sp.wait_ge(s["ea_turned"], b.older)
                for a in (0, 1):
                    sp.dma_start(ean[:, b.u].rearrange("p (k a) f -> p a k f", a=2)[:, a],
                                 ea_d[bass.ds(b.i * BE + a * GRP, GRP), :].rearrange("(k p) f -> p k f", p=P)).then_inc(ea_in[b.u], 16)

            staged(sp, BODIES, (1, load))
            sp.wait_ge(flags_in, 32)

        @block.gpsimd
        def _(pool):
            pool.wait_ge(lists, 1)
            pool.wait_ge(g_clear, 1)

            def ready(b):
                pool.wait_ge(s["act_in"], b.older)
                nc.gpsimd.tensor_copy(gi[:, b.u, :], dsti[:, bass.ds(b.i * ET, ET)]).then_inc(s["copied"], 1)
                wait_apart(pool, passed, (s["copied"], b.now))

            def ready_to_add(b):
                pool.wait_ge(agg_zeroed, 16 * CLEARS)
                wait_apart(pool, passed, (s["addrs"], b.now), (s["summed"], b.now))

            def add_one(k):
                def step(b):
                    pool.indirect_dma_start(out=agg_d, out_offset=bass.IndirectOffsetOnAxis(ap=addi[:, b.u, k:k + 1], axis=0),
                                            in_=sums[:, b.u, k, :], in_offset=None, compute_op=ALU.add).then_inc(one_added[k], 16)
                return step

            def gather_one(k):
                def step(b):
                    pool.indirect_dma_start(out=G[:, b.u, k, :], out_offset=None, in_=x,
                                            in_offset=bass.IndirectOffsetOnAxis(ap=gi[:, b.u, k:k + 1], axis=0),
                                            bounds_check=N - 1, oob_is_err=False).then_inc(gathered[b.u], 16)
                return step

            def landed(k):
                def step(b):
                    wait_apart(pool, passed, (one_added[k], b.value("adds", (b.i + 1) * 16)))
                return step

            def all_added(b):
                pool.sem_inc(s["added"], 1)

            steps = [(2, ready), (0, ready_to_add)]
            for k in range(ET):
                steps += [(0, add_one(k)), (2, gather_one(k)), (0, landed(k))]
            staged(pool, BODIES, *steps, (0, all_added))

        @block.scalar
        def _(act):
            assert load_weights(act, v, weights_in) == LOADS
            nc.scalar.preload_act_table_set(ACT_SET)

            def front(b):
                act.wait_ge(s["ea_turned"], b.now)
                act.wait_ge(eat_out[b.u], b.in2())
                nc.scalar.copy(eat[:, b.u, :], PS[3][0:2 * EF, 0:GRP]).then_inc(s["eat_set"], 1)
                norm_rstd(nc, act, t, s, b, ET, epsc)
                act.wait_ge(s["eat_set"], b.now)
                act.dma_start(eat_d[bass.ds(b.i, 1)].rearrange("o f c -> (o f) c"), eat[:, b.u, :]).then_inc(eat_out[b.u], 16)

            def back(b):
                act.wait_ge(s["selected"], b.now)
                act.wait_ge(s["added"], b.older)
                nc.scalar.copy(sums[:, b.u].rearrange("p k f -> p (k f)"), PS[4][:]).then_inc(s["summed"], 1)

            staged(act, BODIES, (0, back), (1, front))
            act.wait_ge(eat_out[0], 16 * ((BODIES + 1) // 2 + 1))
            act.wait_ge(eat_out[1], 16 * (BODIES // 2 + 1))

        @block.vector
        def _(dve):
            chain = [0]

            def link(ins):
                chain[0] += 1
                ins.then_inc(dchain, 1)
                dve.wait_ge(dchain, chain[0])

            nc.vector.memset(G[:], 0.0).then_inc(g_clear, 1)
            dve.wait_ge(raw_in, 128)
            nc.vector.tensor_copy(rowf["src"][:], raw["src"][:])
            nc.vector.tensor_copy(rowf["dst"][:], raw["cur"][:])
            nc.vector.tensor_tensor(rowf["flag"][:], raw["cur"][:], raw["prv"][:], ALU.is_equal)
            link(nc.vector.tensor_tensor(rowf["eq"][:], raw["cur"][:], raw["nxt"][:], ALU.is_equal))
            link(nc.vector.scalar_tensor_tensor(rowf["last"][:], rowf["eq"][:], float(FAR), rowf["dst"][:], ALU.mult, ALU.add))
            nc.vector.memset(junk[:], 0.0).then_inc(dchain, 1)
            chain[0] += 1
            dve.wait_ge(turned, 1)
            for to, n in ((srci, 0), (srcf, 0), (dsti, 1), (lasti, 2)):
                nb = BODIES
                last = nc.vector.tensor_copy(to[:].rearrange("p (b k a) -> p b a k", b=nb, a=2),
                                             PS[n][:, 0:TILES].rearrange("p (b a k) -> p b a k", b=nb, a=2))
            last.then_inc(lists, 1)
            dve.wait_ge(lists, 1)

            def front(b):
                nc.vector.tensor_copy(sc[:], srcf[:, bass.ds(b.i * ET, ET)]).then_inc(s["sc_set"], 1)
                dve.wait_ge(s["sc_set"], b.now)
                dve.wait_ge(src_in[b.u], b.in2())
                dve.wait_ge(s["selected"], b.prev)
                for k in range(ET):
                    at = (k % 2) * GRP + (k // 2) * P
                    last = nc.vector.tensor_scalar(eq[:, k, :], srcbc[:, b.u, at:at + P], sc[:, k:k + 1], None, ALU.is_equal)
                last.then_inc(s["eqs"], 1)
                dve.wait_ge(s["eqs"], b.now)
                for k in range(ET):
                    last = nc.vector.tensor_tensor_reduce(out=junk[:, k, :], in0=eq[:, k, :], in1=tril[:], scale=1.0, scalar=0.0,
                                                          op0=ALU.mult, op1=ALU.add, accum_out=cnt[:, k:k + 1])
                last.then_inc(s["cnts"], 1)
                nc.vector.tensor_scalar(okm[:], sc[:], float(N), None, ALU.is_lt).then_inc(s["oks"], 1)
                dve.wait_ge(s["cnts"], b.now)
                dve.wait_ge(s["oks"], b.now)
                nc.vector.scalar_tensor_tensor(first[:], cnt[:], 0.5, okm[:], ALU.is_lt, ALU.mult).then_inc(s["firsts"], 1)
                dve.wait_ge(s["firsts"], b.now)
                nc.vector.scalar_tensor_tensor(rel[:], sc[:], spare[:, 0:1], first[:], ALU.subtract, ALU.mult).then_inc(s["rels"], 1)
                dve.wait_ge(s["rels"], b.now)
                dve.wait_ge(s["added"], b.older)
                nc.vector.tensor_scalar(addi[:, b.u, :], rel[:], spare[:, 0:1], None, ALU.add).then_inc(s["addrs"], 1)
                dve.wait_ge(gathered[b.u], b.in2(8))
                norm_stats(nc, dve, t, s, b, G[:, b.u], 0, ET).then_inc(s["stats"], 1)
                norm_moments(nc, dve, t, s, b, ET)
                nc.vector.scalar_tensor_tensor(t["ctr"][:], over(t["tw"][:], F), -0.5, G[:, b.u], ALU.mult, ALU.add).then_inc(s["centred"], 1)
                dve.wait_ge(s["centred"], b.now)
                dve.wait_ge(s["rstd"], b.now)
                nc.vector.scalar_tensor_tensor(H[:], t["ctr"][:], 0.0, over(t["rs"][:], F), ALU.max, ALU.mult).then_inc(s["act_in"], 1)

            staged(dve, BODIES, (1, front))

            dve.wait_ge(weights_in, 16 * LOADS)
            for l in range(L):
                nc.vector.tensor_scalar(ceng[:, l, :], cen[:], gcol[:, l:l + 1], None, ALU.mult)
            link(nc.vector.tensor_tensor(rds[:], rd[:, 0, :], rd[:, 1, :], ALU.mult))
            for l in range(L):
                nc.vector.tensor_scalar(wall[:, l, E2_C:E2_C + HID], wall[:, l, E2_C:E2_C + HID], rds[:, l:l + 1], None, ALU.mult)
                last = nc.vector.tensor_scalar(wall[:, l, BIAS_C + 3:BIAS_C + 4], wall[:, l, BIAS_C + 3:BIAS_C + 4], rds[:, l:l + 1], None, ALU.mult)
            link(last)
            nc.vector.tensor_copy(wcur[:], wall[:, 0, :])
            dve.wait_ge(cenb_mm, 1)
            nc.vector.tensor_copy(cenb[:], PS[5][:, 0:L])

        @block.tensor
        def _(pe):
            pe.wait_ge(dchain, 2)
            for n, k in enumerate(("src", "dst", "last")):
                for h in (0, 1):
                    last = nc.tensor.transpose(PS[n][:, h * HT:(h + 1) * HT], rowf[k][:, h, :], ident[0:HT, 0:HT])
            last.then_inc(turned, 1)

            def front(b):
                wait_apart(pe, pe_passed, (ea_in[b.u], b.in2(2)), (s["eat_set"], b.prev))
                for k in range(ET // 2):
                    last = nc.tensor.transpose(PS[3][0:2 * EF, k * P:(k + 1) * P],
                                               ean[:, b.u, 2 * k:2 * k + 2, :].rearrange("p a f -> p (a f)"), ident[:])
                last.then_inc(s["ea_turned"], 1)

            def back(b):
                pe.wait_ge(s["act_in"], b.now)
                pe.wait_ge(s["summed"], b.prev)
                for k in range(ET):
                    last = nc.tensor.matmul(PS[4][:, k * F:(k + 1) * F], eq[:, k, :], H[:, k, :], start=True, stop=True)
                last.then_inc(s["selected"], 1)

            staged(pe, BODIES, (0, back), (1, front))
            pe.wait_ge(weights_in, 16 * LOADS)
            nc.tensor.matmul(PS[5][:, 0:L], cen[:], bcol[:], start=True, stop=True).then_inc(cenb_mm, 1)


def first_mlp(nc, v):
    x, agg_d, map_d, x1_d = (v[k] for k in ("x", "agg_d", "map_d", "x1_d"))
    ident, epsc, w10, w20, b10, b20 = (v[k] for k in ("ident", "epsc", "w10", "w20", "b10", "b20"))
    srci, lasti, rowi, pidx, PS, PS2 = (v[k] for k in ("srci", "lasti", "rowi", "pidx", "PS", "PS2"))
    BN = P * NB
    BLK = FULL + 1
    with semaphores(nc, "fm_") as sem, ExitStack() as ctx:
        def sb(name, shape, dt=fp32):
            return ctx.enter_context(nc.sbuf_tensor(name, shape, dt))

        X = sb("fm_X", [P, 4, NB, F])
        A = sb("fm_A", [P, 4, NB, F])
        H = sb("fm_H", [P, NB, F])
        HA = sb("fm_HA", [P, NB, F])
        HT_ = sb("fm_HT", [P, NB // 2 * P])
        OT = sb("fm_OT", [P, 512])
        R = sb("fm_R", [P, 2, 512])
        Y = sb("fm_Y", [P, 2, NB, F])
        pi = sb("fm_pi", [P, 2, ET], i32)
        pv = sb("fm_pv", [P, 2, ET], i32)
        t = norm_tiles(sb, NB, "fm")

        x_in = [sem(f"x_in{w}") for w in range(4)]
        y_out = [sem("y_out0"), sem("y_out1")]
        mapped = [v["pool_sem"](f"mapped{u}") for u in (0, 1)]
        looked = [v["pool_sem"](f"fm_looked{u}") for u in (0, 1)]
        body_sems = NORM_SEMS + ("act_in", "with_sums", "turned", "turned_set", "hidden", "hidden_set", "mlp", "out_set", "natural", "sum_set")
        s = {k: sem(k) for k in body_sems}
        map_sems = ("map_idx", "map_sent", "look_idx", "looked_set")
        s |= {k: sem(k) for k in map_sems}
        passed = sem("pool_passed")
        yclear = sem("yclear")

        block = ctx.enter_context(nc.Block())

        def rows(b):
            if isinstance(b.i, int) and b.i == FULL:
                return slice(FULL * BN, N), TAIL
            return bass.ds(b.i * BN, BN), P

        def nparts(b):
            return TAIL if isinstance(b.i, int) and b.i == FULL else P

        @block.sync
        def _(sp):
            for k in s.values():
                sp.sem_inc(k, CREDIT)

            def load(b):
                r, n = rows(b)
                sp.wait_ge(s["sum_set"], b.oldest)
                sp.dma_start(X[0:n, b.w], x[r, :].rearrange("(p g) f -> p g f", g=NB)).then_inc(x_in[b.w], 16)
                sp.dma_start(A[0:n, b.w], agg_d[r, :].rearrange("(p g) f -> p g f", g=NB)).then_inc(x_in[b.w], 16)

            def store(b):
                r, n = rows(b)
                sp.wait_ge(s["sum_set"], b.now)
                sp.dma_start(x1_d[r, :].rearrange("(p g) f -> p g f", g=NB), Y[0:n, b.u]).then_inc(y_out[b.u], 16)

            sp.wait_ge(yclear, 1)
            for u in (0, 1):
                sp.dma_start(x1_d[u * BN:(u + 1) * BN, :].rearrange("(p g) f -> p g f", g=NB), Y[:, u]).then_inc(y_out[u], 16)
                sp.wait_ge(y_out[u], 16)
            staged(sp, BLK, (3, load), (0, store))
            sp.wait_ge(y_out[0], 16 * (BLK // 2 + 1))
            sp.wait_ge(y_out[1], 16 * (BLK // 2 + 1))

        @block.vector
        def _(dve):
            nc.vector.memset(Y[:], 0.0).then_inc(yclear, 1)

            def front(b):
                n = nparts(b)
                dve.wait_ge(x_in[b.w], b.in4(2))
                norm_stats(nc, dve, t, s, b, X[:, b.w], 0, NB, n).then_inc(s["stats"], 1)
                norm_moments(nc, dve, t, s, b, NB, n)
                nc.vector.scalar_tensor_tensor(t["ctr"][0:n], over(t["tw"][0:n], F), -0.5, X[0:n, b.w], ALU.mult, ALU.add).then_inc(s["centred"], 1)

            def relu_norm(b):
                n = nparts(b)
                dve.wait_ge(s["centred"], b.now)
                dve.wait_ge(s["rstd"], b.now)
                nc.vector.scalar_tensor_tensor(H[0:n], t["ctr"][0:n], 0.0, over(t["rs"][0:n], F), ALU.max, ALU.mult).then_inc(s["act_in"], 1)

            def add_sums(b):
                n = nparts(b)
                dve.wait_ge(s["act_in"], b.now)
                dve.wait_ge(s["turned"], b.prev)
                nc.vector.tensor_tensor(HA[0:n], H[0:n], A[0:n, b.w], ALU.add).then_inc(s["with_sums"], 1)

            def back(b):
                n = nparts(b)
                dve.wait_ge(s["natural"], b.now)
                dve.wait_ge(y_out[b.u], b.in2())
                nc.vector.tensor_tensor(Y[0:n, b.u].rearrange("p g f -> p (g f)"), PS[3][0:n, :],
                                        X[0:n, b.w].rearrange("p g f -> p (g f)"), ALU.add).then_inc(s["sum_set"], 1)

            staged(dve, BLK, (2, front), (2, relu_norm), (2, add_sums), (0, back))

        @block.gpsimd
        def _(pool):
            def fill_map(b):
                pool.wait_ge(s["map_sent"], b.older)
                nc.gpsimd.tensor_copy(pi[:, b.u, :], lasti[:, bass.ds(b.i * ET, ET)])
                nc.gpsimd.tensor_copy(pv[:, b.u, :], rowi[:, bass.ds(b.i * ET, ET)]).then_inc(s["map_idx"], 1)
                wait_apart(pool, passed, (s["map_idx"], b.now))
                for k in range(ET):
                    pool.indirect_dma_start(out=map_d, out_offset=bass.IndirectOffsetOnAxis(ap=pi[:, b.u, k:k + 1], axis=0),
                                            in_=pv[:, b.u, k:k + 1], in_offset=None,
                                            bounds_check=N - 1, oob_is_err=False).then_inc(mapped[b.u], 16)

            def filled(b):
                pool.wait_ge(mapped[b.u], b.in2(ET))
                pool.sem_inc(s["map_sent"], 1)

            def look(b):
                pool.wait_ge(s["looked_set"], b.older)
                nc.gpsimd.tensor_copy(pi[:, b.u, :], srci[:, bass.ds(b.i * ET, ET)])
                nc.gpsimd.memset(pv[:, b.u, :], FAR).then_inc(s["look_idx"], 1)
                wait_apart(pool, passed, (s["look_idx"], b.now))
                for k in range(ET):
                    pool.indirect_dma_start(out=pv[:, b.u, k:k + 1], out_offset=None, in_=map_d,
                                            in_offset=bass.IndirectOffsetOnAxis(ap=pi[:, b.u, k:k + 1], axis=0),
                                            bounds_check=N - 1, oob_is_err=False).then_inc(looked[b.u], 16)

            def found(b):
                pool.wait_ge(looked[b.u], b.in2(ET))
                nc.gpsimd.tensor_copy(pidx[:, 0, bass.ds(b.i * ET, ET)], pv[:, b.u, :]).then_inc(s["looked_set"], 1)

            staged(pool, BODIES, (1, fill_map), (0, filled))
            staged(pool, BODIES, (1, look), (0, found))

        @block.scalar
        def _(act):
            nc.scalar.preload_act_table_set(ACT_SET)

            def rstd(b):
                norm_rstd(nc, act, t, s, b, NB, epsc, nparts(b))

            def turned(b):
                n = nparts(b)
                act.wait_ge(s["turned"], b.now)
                act.wait_ge(s["hidden"], b.prev)
                nc.scalar.copy(HT_[:, 0:4 * n], PS[0][:, 0:4 * n]).then_inc(s["turned_set"], 1)

            def back(b):
                n = nparts(b)
                act.wait_ge(s["hidden"], b.now)
                act.wait_ge(s["mlp"], b.prev)
                nc.scalar.activation(R[:, :, 0:4 * n], PS2[:].rearrange("p (a c) -> p a c", a=2)[:, :, 0:4 * n], ACT.Relu,
                                     bias=b10[:, 0:1]).then_inc(s["hidden_set"], 1)

            def out_turned(b):
                n = nparts(b)
                act.wait_ge(s["mlp"], b.now)
                act.wait_ge(s["natural"], b.prev)
                nc.scalar.activation(OT[:, 0:4 * n], PS[2][:, 0:4 * n], ACT.Identity, bias=b20[:, 0:1]).then_inc(s["out_set"], 1)

            staged(act, BLK, (1, turned), (0, out_turned), (2, rstd), (1, back))

        @block.tensor
        def _(pe):
            def turn(b):
                n = nparts(b)
                pe.wait_ge(s["with_sums"], b.now)
                pe.wait_ge(s["turned_set"], b.prev)
                for k in range(NB // 2):
                    last = nc.tensor.transpose(PS[0][:, k * n:(k + 1) * n],
                                               HA[0:n, 2 * k:2 * k + 2, :].rearrange("p a f -> p (a f)"), ident[0:n, 0:n])
                last.then_inc(s["turned"], 1)

            def up(b):
                n = nparts(b)
                pe.wait_ge(s["turned_set"], b.now)
                pe.wait_ge(s["hidden_set"], b.prev)
                for a in (0, 1):
                    last = nc.tensor.matmul(PS2[:, a * 512:a * 512 + 4 * n], w10[a * F:(a + 1) * F, :],
                                            HT_[a * F:(a + 1) * F, 0:4 * n], start=True, stop=True)
                last.then_inc(s["hidden"], 1)

            def back(b):
                n = nparts(b)
                pe.wait_ge(s["hidden_set"], b.now)
                pe.wait_ge(s["out_set"], b.prev)
                for a in (0, 1):
                    last = nc.tensor.matmul(PS[2][a * F:(a + 1) * F, 0:4 * n], w20[:], R[:, a, 0:4 * n], start=True, stop=True)
                last.then_inc(s["mlp"], 1)

            def turn_back(b):
                n = nparts(b)
                pe.wait_ge(s["out_set"], b.now)
                pe.wait_ge(s["sum_set"], b.prev)
                for k in range(NB // 2):
                    last = nc.tensor.transpose(PS[3][0:n, k * 2 * F:(k + 1) * 2 * F], OT[:, k * n:(k + 1) * n], ident[:])
                last.then_inc(s["natural"], 1)

            staged(pe, BLK, (1, turn), (0, back), (1, up), (0, turn_back))


def layers(nc, v):
    x1_d, map_d, st_d, st_rows, xd_d, eat_d, out = (v[k] for k in ("x1_d", "map_d", "st_d", "st_rows", "xd_d", "eat_d", "out"))
    ident, cen, avg, ceng, cenb, epsc, gcol, bcol = (v[k] for k in ("ident", "cen", "avg", "ceng", "cenb", "epsc", "gcol", "bcol"))
    wall, wcur, flags, srci, dsti, lasti, pidx = (v[k] for k in ("wall", "wcur", "flags", "srci", "dsti", "lasti", "pidx"))
    PS, PS2 = v["PS"], v["PS2"]
    NORMS = L + 1
    S2 = 2 * ET
    with semaphores(nc, "ly_", clear=False) as sem, ExitStack() as ctx:
        def sb(name, shape, dt=fp32):
            return ctx.enter_context(nc.sbuf_tensor("ly_" + name, shape, dt))

        X1 = sb("X1", [P, 4, S2, F])
        ST = sb("ST", [P, 4, S2, F])
        NS = sb("NS", [P, 2, S2, F])
        EAT = sb("EAT", [2 * EF, 4, GRP])
        XT = sb("XT", [P, GRP])
        HB = sb("HB", [P, 2, GRP])
        E1 = sb("E1", [P, GRP])
        E2 = sb("E2", [P, GRP])
        MSG = sb("MSG", [P, GRP])
        AG = sb("AG", [P, GRP])
        CAR = sb("CAR", [P, 1])
        CARB = sb("CARB", [P, 1])
        zi = sb("zi", [P, S2, F])
        gi = sb("gi", [P, 4, S2], i32)
        li = sb("li", [P, 2, ET], i32)
        XD = sb("XD", [P, 2, ET, F])
        t0 = norm_tiles(lambda n, s_, *a: sb(n, s_, *a), S2, "t0")
        t1 = norm_tiles(lambda n, s_, *a: sb(n, s_, *a), S2, "t1")
        XN = sb("XN", [P, 4, NB, F])
        Y = sb("Y", [P, NORMS + 1, CC])
        SQ = sb("SQ", [P, 2, CC])
        LV = sb("LV", [P, 2, CC])
        RV = sb("RV", [P, 2, CC])
        FT = sb("FT", [P, CC])
        ON = sb("ON", [P, 2, NB, F])

        x1_in = [v["pool_sem"](f"x1_in{w}") for w in range(4)]
        xd_out = [sem(f"xd_out{w}") for w in range(4)]
        st_in = [sem(f"st_in{w}") for w in range(4)]
        looked = [v["pool_sem"](f"looked{w}") for w in range(4)]
        ea_in = [sem(f"ea_in{w}") for w in range(4)]
        st_out = [sem("st_out0"), sem("st_out1")]
        xd_in = [sem("xd_in0"), sem("xd_in1")]
        scattered = [v["pool_sem"](f"scattered{u}") for u in (0, 1)]
        xn_in = [sem(f"xn_in{w}") for w in range(4)]
        on_out = [sem("on_out0"), sem("on_out1")]
        edge_sems = ("idx", "turned", "xt", "e_up", "e1", "e1_leaky", "hidden", "hb", "hb_leaky", "e_down", "e2", "mlp", "msg", "scan_a",
                     "shift_a", "carb", "scan_b", "shift_b", "car", "back", "sum", "scaled", "gained", "done")
        s = {k: sem(k) for k in edge_sems + NORM_SEMS}
        s0 = {k: sem("first_" + k) for k in NORM_SEMS + ("ready",)}
        sl = {k: sem("last_" + k) for k in ("idx", "final", "gone")}
        node_sems = ("in", "first", "aff", "out", "sum")
        norm_sems = tuple((k, q) for q in range(NORMS) for k in ("centred", "squared", "var", "log", "rstd", "normed"))
        sn = {k: sem("n_" + (k if isinstance(k, str) else f"{k[0]}{k[1]}")) for k in node_sems + norm_sems}
        CHAIN_STEPS = ((2, 2), (0, 3), (5, 1), (3, 2), (1, 3), (4, 2))
        AHEAD = dict(CHAIN_STEPS)
        PAIR = {q: k % 2 for k, (q, _) in enumerate(CHAIN_STEPS)}
        EDGE_IN, EDGE_OUT = PS[0], PS[1]
        CENTRED, VAR = (PS[2], PS[3]), (PS[4], PS[5])

        def bank_free(q, b, what):
            k = [x for x, _ in CHAIN_STEPS].index(q)
            q2, ahead = CHAIN_STEPS[k - 2]
            return sn[(what, q2)], b.of(ahead - AHEAD[q] - (1 if k < 2 else 0))
        cleared = sem("cleared")
        passed, pe_passed = sem("pool_passed"), sem("pe_passed")
        weights = sem("weights")

        block = ctx.enter_context(nc.Block())

        def row(c, G):
            return wcur[:, c:c + F].rearrange("p (o f) -> p o f", o=1).to_broadcast([P, G, F])

        def state_rows(b):
            return bass.ds(((b.layer % 2) * BODIES + b.i) * P, P)

        def before_rows(b):
            return bass.ds((((b.layer + 1) % 2) * BODIES + b.i) * P, P)

        def node_rows(b):
            return bass.ds((b.layer * BODIES + b.i) * CHAIN, CHAIN)

        def all_layers(eng, begin, first, middle, last):
            staged(eng, BODIES, *first, layer=0)
            with eng.Fori(1, L - 1) as l:
                begin(l)
                staged(eng, BODIES, *middle, layer=l)
            begin(L - 1)
            staged(eng, BODIES, *last, layer=L - 1)

        @block.sync
        def _(sp):
            for k in s.values():
                sp.sem_inc(k, CREDIT)
            for k in (*s0.values(), *sl.values(), *sn.values()):
                sp.sem_inc(k, CREDIT)
            sp.wait_ge(cleared, 1)
            for w in range(4):
                sp.dma_start(xd_d[w * P:(w + 1) * P, :], X1[:, w, ET:, :].rearrange("p g f -> p (g f)")).then_inc(xd_out[w], 16)
                sp.wait_ge(xd_out[w], 16)
            for u in (0, 1):
                sp.dma_start(st_d[u * P:(u + 1) * P, :], NS[:, u].rearrange("p g f -> p (g f)")).then_inc(st_out[u], 16)
                sp.wait_ge(st_out[u], 16)
                sp.dma_start(out[u * CHAIN:(u + 1) * CHAIN, :].rearrange("(p g) f -> p g f", g=NB), ON[0:CP, u]).then_inc(on_out[u], 16)
                sp.wait_ge(on_out[u], 16)

            def load_ea(b):
                sp.wait_ge(s["e_up"], b.oldest)
                sp.dma_start(EAT[:, b.w, :], eat_d[bass.ds(b.i, 1)].rearrange("o f c -> (o f) c")).then_inc(ea_in[b.w], 16)

            def load_state(b):
                sp.wait_ge(s["centred"], b.oldest)
                for u in (0, 1):
                    sp.wait_ge(st_out[u], b.value(("stored", u), b.layer * (16 * ((BODIES + 1 - u) // 2)) + 16))
                sp.dma_start(ST[:, b.w].rearrange("p g f -> p (g f)"), st_d[before_rows(b), :]).then_inc(st_in[b.w], 16)

            def load_nodes(b):
                sp.wait_ge(sn["sum"], b.oldest)
                sp.dma_start(XN[0:CP, b.w], x1_d[node_rows(b), :].rearrange("(p g) f -> p g f", g=NB)).then_inc(xn_in[b.w], 16)

            def load_targets(b):
                sp.wait_ge(sl["gone"], b.at(2, L - 1))
                sp.dma_start(XD[:, b.u].rearrange("p g f -> p (g f)"), xd_d[bass.ds(b.i * P, P), :]).then_inc(xd_in[b.u], 16)

            def store_targets(b):
                sp.wait_ge(x1_in[b.w], b.in4(S2))
                sp.dma_start(xd_d[bass.ds(b.i * P, P), :], X1[:, b.w, ET:, :].rearrange("p g f -> p (g f)")).then_inc(xd_out[b.w], 16)

            def store_first(b):
                sp.wait_ge(s["done"], b.now)
                sp.dma_start(st_d.rearrange("(r a) f -> a r f", r=2)[bass.ds(b.i * P, P)],
                             NS[:, b.u].rearrange("p (o g) f -> p o (g f)", o=1).to_broadcast([P, 2, S2 * F])).then_inc(st_out[b.u], 16)

            def store_state(b):
                sp.wait_ge(s["done"], b.now)
                sp.dma_start(st_d[state_rows(b), :], NS[:, b.u].rearrange("p g f -> p (g f)")).then_inc(st_out[b.u], 16)

            def store_nodes(b):
                sp.wait_ge(sn["sum"], b.now)
                sp.dma_start(out[node_rows(b), :].rearrange("(p g) f -> p g f", g=NB), ON[0:CP, b.u]).then_inc(on_out[b.u], 16)

            def begin(l):
                if isinstance(l, int):
                    for w in range(4):
                        sp.wait_ge(xd_out[w], 16 * ((BODIES + 3 - w) // 4) + 16)

            all_layers(sp, begin,
                       [(4, load_ea), (4, load_nodes), (2, store_targets), (0, store_first), (1, store_nodes)],
                       [(4, load_ea), (4, load_nodes), (4, load_state), (0, store_state), (1, store_nodes)],
                       [(4, load_ea), (4, load_state), (1, load_targets)])

        @block.gpsimd
        def _(pool):
            pool.wait_ge(cleared, 1)

            def first_idx(b):
                pool.wait_ge(s0["centred"], b.oldest)
                nc.gpsimd.tensor_copy(gi[:, b.w, 0:ET], srci[:, bass.ds(b.i * ET, ET)])
                nc.gpsimd.tensor_copy(gi[:, b.w, ET:], dsti[:, bass.ds(b.i * ET, ET)]).then_inc(s["idx"], 1)

            def gather_x1(b):
                wait_apart(pool, passed, (s["idx"], b.now), (xd_out[b.w], b.in4()))
                for k in range(S2):
                    pool.indirect_dma_start(out=X1[:, b.w, k, :], out_offset=None, in_=x1_d,
                                            in_offset=bass.IndirectOffsetOnAxis(ap=gi[:, b.w, k:k + 1], axis=0),
                                            bounds_check=N - 1, oob_is_err=False).then_inc(x1_in[b.w], 16)

            def idx(b):
                pool.wait_ge(s["turned"], b.oldest)
                nc.gpsimd.tensor_copy(gi[:, b.w, 0:ET], pidx[:, bass.ds((b.layer + 1) % 2, 1), bass.ds(b.i * ET, ET)].rearrange("p o k -> p (o k)")).then_inc(s["idx"], 1)

            def look(b):
                wait_apart(pool, passed, (s["idx"], b.now), (st_in[b.w], b.in4(skip=1)))
                for k in range(ET):
                    pool.indirect_dma_start(out=ST[:, b.w, k, :], out_offset=None, in_=st_rows,
                                            in_offset=bass.IndirectOffsetOnAxis(ap=gi[:, b.w, k:k + 1], axis=0),
                                            bounds_check=2 * ROWS - 1, oob_is_err=False).then_inc(looked[b.w], 16)

            def gain(b):
                pool.wait_ge(s["scaled"], b.now)
                nc.gpsimd.tensor_tensor(zi[:], zi[:], row(G_C, S2), ALU.mult).then_inc(s["gained"], 1)

            def shift(b):
                pool.wait_ge(s["gained"], b.now)
                pool.wait_ge(st_out[b.u], b.in2())
                nc.gpsimd.tensor_tensor(NS[:, b.u], zi[:], row(B_C, S2), ALU.add).then_inc(s["done"], 1)

            def last_idx(b):
                nc.gpsimd.tensor_copy(li[:, b.u, :], lasti[:, bass.ds(b.i * ET, ET)]).then_inc(sl["idx"], 1)

            def scatter(b):
                wait_apart(pool, passed, (sl["idx"], b.at(0, L - 1)), (sl["final"], b.at(0, L - 1)))
                for k in range(ET):
                    pool.indirect_dma_start(out=out, out_offset=bass.IndirectOffsetOnAxis(ap=li[:, b.u, k:k + 1], axis=0),
                                            in_=XD[:, b.u, k, :], in_offset=None,
                                            bounds_check=N - 1, oob_is_err=False).then_inc(scattered[b.u], 16)

            def scattered_all(b):
                pool.wait_ge(scattered[b.u], b.in2(ET, skip=L - 1))
                pool.sem_inc(sl["gone"], 1)

            def begin(l):
                pool.wait_ge(weights, l + 1)
                if isinstance(l, int):
                    for u in (0, 1):
                        pool.wait_ge(on_out[u], 16 * (L - 1) * ((BODIES + 1 - u) // 2) + 16)

            all_layers(pool, begin, [(0, gain), (0, shift), (3, first_idx), (3, gather_x1)],
                       [(0, gain), (0, shift), (3, idx), (3, look)],
                       [(0, last_idx), (0, scatter), (3, idx), (3, look), (0, scattered_all)])

        @block.tensor
        def _(pe):
            def turn(ready):
                def step(b):
                    pe.wait_ge(*ready(b))
                    pe.wait_ge(s["e2"], b.now)
                    for k in range(ET // 2):
                        last = nc.tensor.transpose(EDGE_IN[:, k * P:(k + 1) * P],
                                                   ST[:, b.w, 2 * k:2 * k + 2, :].rearrange("p a f -> p (a f)"), ident[:])
                    last.then_inc(s["turned"], 1)
                return step

            turn_first = turn(lambda b: (s0["ready"], b.now))
            turn_next = turn(lambda b: (looked[b.w], b.in4(ET, skip=1)))

            def e_up(b):
                pe.wait_ge(ea_in[b.w], b.in4())
                pe.wait_ge(s["xt"], b.prev)
                nc.tensor.matmul(EDGE_IN[:], wcur[0:2 * EF, E1_C:E1_C + HID], EAT[:, b.w, :], start=True, stop=True).then_inc(s["e_up"], 1)

            def up(b):
                pe.wait_ge(s["xt"], b.now)
                pe.wait_ge(s["hb"], b.prev)
                for a in (0, 1):
                    last = nc.tensor.matmul(PS2[:, a * GRP:(a + 1) * GRP], wcur[a * F:(a + 1) * F, W1_C:W1_C + HID],
                                            XT[a * F:(a + 1) * F, :], start=True, stop=True)
                last.then_inc(s["hidden"], 1)

            def e_down(b):
                pe.wait_ge(s["e1_leaky"], b.now)
                nc.tensor.matmul(EDGE_IN[:], wcur[:, E2_C:E2_C + HID], E1[:], start=True, stop=True).then_inc(s["e_down"], 1)

            def down(b):
                pe.wait_ge(s["hb_leaky"], b.now)
                pe.wait_ge(s["sum"], b.prev)
                for a in (0, 1):
                    last = nc.tensor.matmul(EDGE_OUT[a * F:(a + 1) * F, :], wcur[:, W2_C:W2_C + F], HB[:, a, :], start=True, stop=True)
                last.then_inc(s["mlp"], 1)

            def shift_a(b):
                wait_apart(pe, pe_passed, (s["scan_a"], b.now))
                nc.tensor.matmul(EDGE_OUT[F:P, 0:1], ident[0:F, 0:F], AG[0:F, GRP - 1:GRP], start=True, stop=True).then_inc(s["shift_a"], 1)

            def shift_b(b):
                wait_apart(pe, pe_passed, (s["scan_b"], b.now))
                nc.tensor.matmul(EDGE_OUT[0:F, 0:1], ident[F:P, F:P], AG[F:P, GRP - 1:GRP], start=True, stop=True).then_inc(s["shift_b"], 1)

            def turn_back(b):
                pe.wait_ge(s["car"], b.now)
                for k in range(ET // 2):
                    last = nc.tensor.transpose(EDGE_OUT[:, k * P:(k + 1) * P], AG[:, k * P:(k + 1) * P], ident[:])
                last.then_inc(s["back"], 1)

            def n_in(b):
                pe.wait_ge(xn_in[b.w], b.in4())
                pe.wait_ge(sn[("normed", 4)], b.of(AHEAD[4] - AHEAD[0] - 1))
                for k in range(NB // 2):
                    last = nc.tensor.transpose(CENTRED[1][:, k * CP:(k + 1) * CP],
                                               XN[0:CP, b.w, 2 * k:2 * k + 2, :].rearrange("p a f -> p (a f)"), ident[0:CP, 0:CP])
                last.then_inc(sn["in"], 1)

            def n_c(q):
                def step(b):
                    if q:
                        pe.wait_ge(sn[("normed", q - 1)], b.now)
                        pe.wait_ge(*bank_free(q, b, "normed"))
                    else:
                        pe.wait_ge(sn["first"], b.now)
                    nc.tensor.matmul(CENTRED[PAIR[q]][:, 0:CC], cen[:] if q < 2 else ceng[:, q - 2, :], Y[:, q, :],
                                     start=True, stop=True).then_inc(sn[("centred", q)], 1)
                return step

            def n_v(q):
                def step(b):
                    pe.wait_ge(sn[("squared", q)], b.now)
                    pe.wait_ge(*bank_free(q, b, "log"))
                    if q == CHAIN_STEPS[0][0]:
                        pe.wait_ge(sn["sum"], b.of(AHEAD[NORMS - 1] - AHEAD[q] - 1))
                    nc.tensor.matmul(VAR[PAIR[q]][:, 0:CC], avg[:], SQ[:, PAIR[q], :], start=True, stop=True).then_inc(sn[("var", q)], 1)
                return step

            def n_out(b):
                pe.wait_ge(sn["aff"], b.now)
                pe.wait_ge(sn[("log", 1)], b.of(AHEAD[1] - AHEAD[NORMS - 1]))
                for k in range(NB // 2):
                    last = nc.tensor.transpose(VAR[0][0:CP, k * P:(k + 1) * P], FT[:, k * CP:(k + 1) * CP], ident[:])
                last.then_inc(sn["out"], 1)

            def begin(l):
                pe.wait_ge(weights, l + 1)

            def order(turn, nodes):
                if not nodes:
                    return [(1, down), (2, e_up), (1, shift_a), (2, e_down), (1, shift_b), (2, turn), (1, turn_back), (2, up)]
                return [(2, n_c(2)), (1, down), (3, n_in), (2, n_v(2)), (3, n_c(0)), (2, e_up), (3, n_v(0)),
                        (1, n_c(5)), (1, shift_a), (1, n_v(5)), (2, n_c(3)), (2, e_down), (1, shift_b), (2, n_v(3)),
                        (3, n_c(1)), (1, turn_back), (2, turn), (3, n_v(1)), (2, n_c(4)), (2, up), (2, n_v(4)), (1, n_out)]

            all_layers(pe, begin, order(turn_first, True), order(turn_next, True), order(turn_next, False))

        @block.scalar
        def _(act):
            nc.scalar.preload_act_table_set(ACT_SET)

            def bias(c):
                return wcur[:, BIAS_C + c:BIAS_C + c + 1]

            def xt(b):
                act.wait_ge(s["turned"], b.now)
                act.wait_ge(s["hidden"], b.prev)
                nc.scalar.copy(XT[:], EDGE_IN[:]).then_inc(s["xt"], 1)

            def e1(b):
                act.wait_ge(s["e_up"], b.now)
                act.wait_ge(s["e_down"], b.prev)
                nc.scalar.activation(E1[:], EDGE_IN[:], ACT.Identity, bias=bias(1)).then_inc(s["e1"], 1)

            def hb(b):
                act.wait_ge(s["hidden"], b.now)
                act.wait_ge(s["mlp"], b.prev)
                nc.scalar.activation(HB[:].rearrange("p a c -> p (a c)"), PS2[:], ACT.Identity, bias=bias(0)).then_inc(s["hb"], 1)

            def e2(b):
                act.wait_ge(s["e_down"], b.now)
                act.wait_ge(s["msg"], b.prev)
                nc.scalar.activation(E2[:], EDGE_IN[:], ACT.Identity, bias=bias(3)).then_inc(s["e2"], 1)

            def rstd0(b):
                norm_rstd(nc, act, t0, s0, b, S2, epsc)

            def rstd(G):
                return lambda b: norm_rstd(nc, act, t1, s, b, G, epsc)

            def n_first(b):
                act.wait_ge(sn["in"], b.now)
                nc.scalar.copy(Y[:, 0, :], CENTRED[1][:, 0:CC]).then_inc(sn["first"], 1)

            def n_q(q):
                def step(b):
                    act.wait_ge(sn[("centred", q)], b.now)
                    shift = 0.0 if q < 2 else cenb[:, q - 2:q - 1]
                    nc.scalar.activation(SQ[:, PAIR[q], :], CENTRED[PAIR[q]][:, 0:CC], ACT.Square, bias=shift).then_inc(sn[("squared", q)], 1)
                return step

            def n_r(q):
                def step(b):
                    act.wait_ge(sn[("var", q)], b.now)
                    nc.scalar.activation(LV[:, PAIR[q], :], VAR[PAIR[q]][:, 0:CC], ACT.Ln, bias=epsc[:, 0:1]).then_inc(sn[("log", q)], 1)
                    act.wait_ge(sn[("log", q)], b.now)
                    nc.scalar.activation(RV[:, PAIR[q], :], LV[:, PAIR[q], :], ACT.Exp, scale=-0.5).then_inc(sn[("rstd", q)], 1)
                return step

            def n_aff(b):
                act.wait_ge(sn[("normed", NORMS - 1)], b.now)
                act.wait_ge(sn["out"], b.prev)
                nc.scalar.activation(FT[:], Y[:, NORMS, :], ACT.Identity, bias=bcol[:, L - 1:L], scale=gcol[:, L - 1:L]).then_inc(sn["aff"], 1)

            def begin(l):
                act.wait_ge(weights, l + 1)

            def order(first, G, nodes):
                if not nodes:
                    return [(0, rstd(G)), (2, e1), (2, e2), (2, xt), (2, hb)]
                return ([(0, rstd(G)), (2, n_q(2)), (3, n_first), (2, n_r(2)), (3, n_q(0)), (2, e1), (3, n_r(0)), (1, n_q(5)), (1, n_r(5))] + first +
                        [(2, n_q(3)), (2, e2), (2, n_r(3)), (1, n_aff), (3, n_q(1)), (2, xt), (3, n_r(1)),
                         (2, n_q(4)), (2, hb), (2, n_r(4))])

            all_layers(act, begin, order([(2, rstd0)], S2, True), order([], S2, True), order([], ET, False))

        @block.vector
        def _(dve):
            nc.vector.memset(X1[:], 0.0)
            nc.vector.memset(NS[:], 0.0)
            nc.vector.memset(ON[:], 0.0)
            nc.vector.memset(CAR[:], 0.0).then_inc(cleared, 1)
            nc.vector.tensor_scalar(pidx[:, 1, :], pidx[:, 0, :], float(ROWS), None, ALU.add).then_inc(weights, 1)

            def enter(b):
                dve.wait_ge(x1_in[b.w], b.in4(S2))
                norm_stats(nc, dve, t0, s0, b, X1[:, b.w], 0, S2).then_inc(s0["stats"], 1)
                norm_moments(nc, dve, t0, s0, b, S2)
                nc.vector.scalar_tensor_tensor(t0["ctr"][:], over(t0["tw"][:], F), -0.5, X1[:, b.w], ALU.mult, ALU.add).then_inc(s0["centred"], 1)

            def entered(b):
                dve.wait_ge(s0["centred"], b.now)
                dve.wait_ge(s0["rstd"], b.now)
                dve.wait_ge(s["turned"], b.older)
                nc.vector.scalar_tensor_tensor(ST[:, b.w], t0["ctr"][:], 0.0, over(t0["rs"][:], F), ALU.max, ALU.mult).then_inc(s0["ready"], 1)

            def e1_leaky(b):
                dve.wait_ge(s["e1"], b.now)
                nc.vector.scalar_tensor_tensor(E1[:], E1[:], SLOPE, E1[:], ALU.mult, ALU.max).then_inc(s["e1_leaky"], 1)

            def hb_leaky(b):
                dve.wait_ge(s["hb"], b.now)
                nc.vector.scalar_tensor_tensor(HB[:], HB[:], SLOPE, HB[:], ALU.mult, ALU.max).then_inc(s["hb_leaky"], 1)

            def msg(b):
                dve.wait_ge(s["mlp"], b.now)
                dve.wait_ge(s["e2"], b.now)
                nc.vector.scalar_tensor_tensor(MSG[:], EDGE_OUT[:], wcur[:, BIAS_C + 2:BIAS_C + 3], E2[:], ALU.add, ALU.mult).then_inc(s["msg"], 1)

            def scan_a(b):
                dve.wait_ge(s["msg"], b.now)
                dve.wait_ge(s["car"], b.prev)
                dve.wait_ge(s["back"], b.prev)
                nc.vector.tensor_tensor_scan(AG[0:F, :], flags[0:F, bass.ds(b.i * GRP, GRP)], MSG[0:F, :], CAR[0:F, 0:1],
                                             ALU.mult, ALU.add).then_inc(s["scan_a"], 1)

            def scan_b(b):
                dve.wait_ge(s["shift_a"], b.now)
                nc.vector.tensor_copy(CARB[F:P, :], EDGE_OUT[F:P, 0:1]).then_inc(s["carb"], 1)
                dve.wait_ge(s["carb"], b.now)
                nc.vector.tensor_tensor_scan(AG[F:P, :], flags[F:P, bass.ds(b.i * GRP, GRP)], MSG[F:P, :], CARB[F:P, 0:1],
                                             ALU.mult, ALU.add).then_inc(s["scan_b"], 1)

            def car(b):
                dve.wait_ge(s["shift_b"], b.now)
                nc.vector.tensor_copy(CAR[0:F, :], EDGE_OUT[0:F, 0:1]).then_inc(s["car"], 1)

            def stats_sources(ready):
                def step(b):
                    dve.wait_ge(*ready(b))
                    dve.wait_ge(s["var"], b.prev)
                    norm_stats(nc, dve, t1, s, b, ST[:, b.w], 0, ET)
                return step

            def add_sums(b):
                dve.wait_ge(s["back"], b.now)
                nc.vector.tensor_tensor(ST[:, b.w, ET:, :].rearrange("p g f -> p (g f)"), EDGE_OUT[:],
                                        ST[:, b.w, ET:, :].rearrange("p g f -> p (g f)"), ALU.add).then_inc(s["sum"], 1)

            def norm_in(lo, G):
                def step(b):
                    dve.wait_ge(s["sum"], b.now)
                    for g in range(ET):
                        last = nc.vector.bn_stats(t1["st"][:, g + (ET if lo == 0 else 0), :], ST[:, b.w, ET + g, :])
                    last.then_inc(s["stats"], 1)
                    norm_moments(nc, dve, t1, s, b, G)
                return step

            def norm_centre(lo, G):
                def step(b):
                    nc.vector.scalar_tensor_tensor(t1["ctr"][:, 0:G], over(t1["tw"][:, 0:G], F), -0.5, ST[:, b.w, lo:, :],
                                                   ALU.mult, ALU.add).then_inc(s["centred"], 1)
                return step

            def norm_scale(G):
                def step(b):
                    dve.wait_ge(s["centred"], b.now)
                    dve.wait_ge(s["rstd"], b.now)
                    dve.wait_ge(s["done"], b.prev)
                    nc.vector.tensor_tensor(zi[:, 0:G], t1["ctr"][:, 0:G], over(t1["rs"][:, 0:G], F), ALU.mult).then_inc(s["scaled"], 1)
                return step

            def norm_gain(G):
                def step(b):
                    dve.wait_ge(s["scaled"], b.now)
                    nc.vector.tensor_tensor(zi[:, 0:G], zi[:, 0:G], row(G_C, G), ALU.mult).then_inc(s["gained"], 1)
                return step

            def norm_last(b):
                dve.wait_ge(s["gained"], b.now)
                nc.vector.tensor_tensor(zi[:, ET:, :], zi[:, 0:ET], row(B_C, ET), ALU.add).then_inc(s["done"], 1)
                dve.wait_ge(s["done"], b.now)
                dve.wait_ge(xd_in[b.u], b.in2(skip=L - 1))
                nc.vector.tensor_tensor(XD[:, b.u], XD[:, b.u], zi[:, ET:, :], ALU.add).then_inc(sl["final"], 1)

            def n_y(q):
                def step(b):
                    dve.wait_ge(sn[("rstd", q)], b.now)
                    shift = 0.0 if q < 2 else cenb[:, q - 2:q - 1]
                    nc.vector.scalar_tensor_tensor(Y[:, q + 1, :], CENTRED[PAIR[q]][:, 0:CC], shift, RV[:, PAIR[q], :],
                                                   ALU.add if q else ALU.max, ALU.mult).then_inc(sn[("normed", q)], 1)
                return step

            def n_sum(b):
                dve.wait_ge(sn["out"], b.now)
                dve.wait_ge(on_out[b.u], b.in2())
                nc.vector.tensor_tensor(ON[0:CP, b.u].rearrange("p g f -> p (g f)"), VAR[0][0:CP, :],
                                        XN[0:CP, b.w].rearrange("p g f -> p (g f)"), ALU.add).then_inc(sn["sum"], 1)

            def begin(l):
                dve.wait_ge(s["done"], l * BODIES + CREDIT)
                if isinstance(l, int):
                    nc.vector.tensor_copy(wcur[:], wall[:, l, :]).then_inc(weights, 1)
                else:
                    nc.vector.tensor_copy(wcur[:], wall[:, bass.ds(l, 1), :].rearrange("p o c -> p (o c)")).then_inc(weights, 1)

            ready = lambda b: (s0["ready"], b.now)
            found = lambda b: (looked[b.w], b.in4(ET, skip=1))

            def order(enter_, entered_, sources):
                return ([(1, msg), (0, norm_scale(S2)), (2, n_y(2)), (1, scan_a)] + enter_ +
                        [(3, n_y(0)), (2, e1_leaky), (1, scan_b), (1, stats_sources(sources)), (1, n_y(5)), (1, car)] +
                        entered_ + [(2, n_y(3)), (1, add_sums), (1, norm_in(0, S2)), (3, n_y(1)),
                                    (1, norm_centre(0, S2)), (2, hb_leaky), (2, n_y(4)), (1, n_sum)])

            all_layers(dve, begin, order([(2, enter)], [(2, entered)], ready), order([], [], found),
                       [(1, msg), (0, norm_scale(ET)), (1, scan_a), (0, norm_gain(ET)), (2, e1_leaky), (1, scan_b), (0, norm_last), (1, car),
                        (1, add_sums), (1, norm_in(ET, ET)), (1, norm_centre(ET, ET)), (2, hb_leaky)])


_INS = ['x', 'src', 'dst', 'edge_attr_32', 'L0_gnn_W1', 'L0_gnn_b1', 'L0_gnn_W2', 'L0_gnn_b2', 'L1_gnn_W1',
        'L1_gnn_b1', 'L1_gnn_W2', 'L1_gnn_b2', 'L1_gnn_We1', 'L1_gnn_be1', 'L1_gnn_We2', 'L1_gnn_be2',
        'L1_gnn_res_w', 'L1_gnn_dot_scale', 'L1_gnn_ln_g', 'L1_gnn_ln_b']
_OUTS = [((100000, 64), 'float32')]


def kernel(**inputs):
    import numpy as _np
    import concourse.bacc as _bacc
    from concourse import mybir as _mybir
    from concourse.bass_utils import run_bass_kernel_spmd as _run

    nc = _bacc.Bacc("TRN2", target_bir_lowering=False, num_devices=1)
    arrays, args = {}, []
    for name in _INS:
        a = _np.ascontiguousarray(inputs[name])
        arrays[f"in_{name}_dram"] = a
        args.append(nc.dram_tensor(f"in_{name}_dram", a.shape, _mybir.dt.from_np(a.dtype), kind="ExternalInput").ap())
    for i, (shape, dtype) in enumerate(_OUTS):
        dt = _mybir.dt.from_np(_np.dtype(dtype))
        args.append(nc.dram_tensor(f"out_{i}_dram", shape, dt, kind="ExternalOutput").ap())
    gnn_kernel(nc, *args)
    r = _run(nc, [arrays], core_ids=[0])
    got = tuple(r.results[0][f"out_{i}_dram"] for i in range(len(_OUTS)))
    return got[0]
```
